# Optimizing a Trainium2 kernel written in Bass

```python
import numpy as np
import jax
import jax.numpy as jnp

def _softmax(x, axis=-1):
    return jax.nn.softmax(x, axis=axis)

def _gelu(x):
    return jax.nn.gelu(x, approximate=True)

def _silu(x):
    return jax.nn.silu(x)

def _sigmoid(x):
    return jax.nn.sigmoid(x)

def _layernorm(x, axis=-1, eps=1e-05):
    m = jnp.mean(x, axis=axis, keepdims=True)
    v = jnp.var(x, axis=axis, keepdims=True)
    return (x - m) / jnp.sqrt(v + eps)

def _scatter_add(tgt, idx, src, axis=0):
    return tgt.at[idx].add(src)

def _segment_sum(src, seg, n):
    return jax.ops.segment_sum(src, seg, n)
kernel_name = 'mk_xattn_ffn_d2_seqx_r8_e70cd4'

def setup_inputs(seed: int=0):
    np.random.seed(seed)
    _w = jnp.asarray

    def _rec_inputs():
        import jax
        import jax.numpy as jnp
        _rk = jax.random.key(seed)
        x = 7.22e-05 + 1 * jax.random.normal(jax.random.fold_in(_rk, 1), (8, 128, 128), jnp.float32)
        _lenS = 128 - jax.random.randint(jax.random.fold_in(_rk, 7), (8,), 0, max(1, 128 // 4) + 1, jnp.int32)
        _lenS2 = 128 - jax.random.randint(jax.random.fold_in(_rk, 8), (8,), 0, max(1, 128 // 4) + 1, jnp.int32)
        _ctx_1024P = jax.random.normal(jax.random.fold_in(_rk, 11), (8, 16, 128), jnp.float32)
        _ctx_1024c = jax.random.dirichlet(jax.random.fold_in(_rk, 511), 0.3 * jnp.ones((16,), jnp.float32), (8, 128))
        _ctx_1024t = jnp.einsum('bsk,bkd->bsd', _ctx_1024c, _ctx_1024P)
        _ctx_1024t = _ctx_1024t * jax.lax.rsqrt(jnp.mean(jnp.square(_ctx_1024t)) + 1e-12) * 0.953939
        ctx_1024 = 4.13588e-05 + 0.999923 * (_ctx_1024t + 0.3 * jax.random.normal(jax.random.fold_in(_rk, 611), (8, 128, 128), jnp.float32))
        _validS = jnp.arange(128)[None, :] < _lenS[:, None]
        _validS2 = jnp.arange(128)[None, :] < _lenS2[:, None]
        _causal = jnp.tril(jnp.ones((128, 128), dtype=bool))
        mask_BxSxS2_ik1 = jnp.where(jnp.broadcast_to(_validS2[:, None, :], (8, 128, 128)), 1, 0).astype(jnp.int32)
        mask_1x1xSxS2_ik1 = jnp.where(jnp.broadcast_to(_validS2[0:1, None, None, :], (1, 1, 128, 128)), 1, 0).astype(jnp.int32)
        return (x, ctx_1024, mask_BxSxS2_ik1, mask_1x1xSxS2_ik1)
    x, ctx_1024, mask_BxSxS2_ik1, mask_1x1xSxS2_ik1 = _rec_inputs()

    def _L0_xattn_setup():
        import jax, jax.numpy as jnp
        import numpy as np
        H = 16
        D_MODEL = 128
        D_K = D_MODEL // H
        NEG = -1000000000.0
        key = jax.random.key(seed)
        ks = jax.random.split(key, 9)
        nb, nw = (4, 256)
        Q = jax.random.normal(ks[0], (nb, nw, D_MODEL), dtype=jnp.float32)
        K = jax.random.normal(ks[1], (nb, nw, D_MODEL), dtype=jnp.float32)
        V = jax.random.normal(ks[2], (nb, nw, D_MODEL), dtype=jnp.float32)
        mask = jax.random.randint(ks[3], (nb, nw, nw), 0, 2, dtype=jnp.int32)
        s = 1.0 / np.sqrt(D_MODEL)
        Wq = jax.random.normal(ks[4], (D_MODEL, D_MODEL), dtype=jnp.float32) * s
        Wk = jax.random.normal(ks[5], (D_MODEL, D_MODEL), dtype=jnp.float32) * s
        Wv = jax.random.normal(ks[6], (D_MODEL, D_MODEL), dtype=jnp.float32) * s
        Wo = jax.random.normal(ks[7], (D_MODEL, D_MODEL), dtype=jnp.float32) * s
        return {'Q': Q, 'K': K, 'V': V, 'mask': mask, 'Wq': Wq, 'Wk': Wk, 'Wv': Wv, 'Wo': Wo}
    _L0_xattn_all = _L0_xattn_setup()
    _L0_xattn_in = {k: v for k, v in _L0_xattn_all.items() if k in ('Wq', 'Wk', 'Wv', 'Wo')}
    del _L0_xattn_all

    def _L0_ffn_setup():
        import jax, jax.numpy as jnp
        import numpy as np
        HIDDEN = 128
        INNER = 512

        def _weight_quant(w):
            scale = 1.0 / jnp.clip(jnp.mean(jnp.abs(w)), 1e-05)
            wq = jnp.clip(jnp.round(w * scale), -1.0, 1.0) / scale
            return w + jax.lax.stop_gradient(wq - w)

        def _act_quant(x):
            scale = 127.0 / jnp.clip(jnp.max(jnp.abs(x), axis=-1, keepdims=True), 1e-05)
            xq = jnp.clip(jnp.round(x * scale), -128.0, 127.0) / scale
            return x + jax.lax.stop_gradient(xq - x)

        def _bitlinear(x, w):
            return jnp.einsum('bsi,oi->bso', _act_quant(x), _weight_quant(w))
        key = jax.random.key(seed)
        k0, k1, k2, k3 = jax.random.split(key, 4)
        x = jax.random.normal(k0, (4, 256, HIDDEN), dtype=jnp.float32)
        w_gate = jax.random.normal(k1, (INNER, HIDDEN), dtype=jnp.float32) / np.sqrt(HIDDEN)
        w_up = jax.random.normal(k2, (INNER, HIDDEN), dtype=jnp.float32) / np.sqrt(HIDDEN)
        w_down = jax.random.normal(k3, (HIDDEN, INNER), dtype=jnp.float32) / np.sqrt(INNER)
        return {'x': x, 'w_gate': w_gate, 'w_up': w_up, 'w_down': w_down}
    _L0_ffn_all = _L0_ffn_setup()
    _L0_ffn_in = {k: v for k, v in _L0_ffn_all.items() if k in ('w_gate', 'w_up', 'w_down')}
    del _L0_ffn_all

    def _L1_xattn_setup():
        import jax, jax.numpy as jnp
        import numpy as np
        EMBED = 128
        HEADS = 16
        HEAD_DIM = EMBED // HEADS
        B, S = (4, 256)
        key = jax.random.key(seed)
        ks = jax.random.split(key, 9)
        q = jax.random.normal(ks[0], (B, S, EMBED), dtype=jnp.float32)
        k = jax.random.normal(ks[1], (B, S, EMBED), dtype=jnp.float32)
        v = jax.random.normal(ks[2], (B, S, EMBED), dtype=jnp.float32)
        mask = jax.random.randint(ks[3], (1, 1, S, S), 0, 2, dtype=jnp.int32)
        sc = 1.0 / np.sqrt(HEAD_DIM)
        Wq = jax.random.normal(ks[4], (HEAD_DIM, HEAD_DIM), dtype=jnp.float32) * sc
        Wk = jax.random.normal(ks[5], (HEAD_DIM, HEAD_DIM), dtype=jnp.float32) * sc
        Wv = jax.random.normal(ks[6], (HEAD_DIM, HEAD_DIM), dtype=jnp.float32) * sc
        Wo = jax.random.normal(ks[7], (EMBED, EMBED), dtype=jnp.float32) * (1.0 / np.sqrt(EMBED))
        bo = jax.random.normal(ks[8], (EMBED,), dtype=jnp.float32) * 0.01
        return {'q': q, 'k': k, 'v': v, 'mask': mask, 'Wq': Wq, 'Wk': Wk, 'Wv': Wv, 'Wo': Wo, 'bo': bo}
    _L1_xattn_all = _L1_xattn_setup()
    _L1_xattn_in = {k: v for k, v in _L1_xattn_all.items() if k in ('Wq', 'Wk', 'Wv', 'Wo', 'bo')}
    del _L1_xattn_all

    def _L1_ffn_setup():
        import jax, jax.numpy as jnp
        import numpy as np
        B, S, D, H, E, K = (4, 128, 128, 256, 8, 2)
        key = jax.random.key(seed)
        ks = jax.random.split(key, 5)
        s = 0.02
        return {'x': jax.random.normal(ks[0], (B, S, D), jnp.float32), 'W1': jax.random.normal(ks[1], (E, H, D), jnp.float32) * s, 'b1': jnp.zeros((E, H), jnp.float32), 'W2': jax.random.normal(ks[2], (E, D, H), jnp.float32) * s, 'b2': jnp.zeros((E, D), jnp.float32), 'Wg': jax.random.normal(ks[3], (E, D), jnp.float32) * s, 'bg': jnp.zeros((E,), jnp.float32)}
    _L1_ffn_all = _L1_ffn_setup()
    _L1_ffn_in = {k: v for k, v in _L1_ffn_all.items() if k in ('W1', 'b1', 'W2', 'b2', 'Wg', 'bg')}
    del _L1_ffn_all
    return {'x': x, 'ctx_1024': ctx_1024, 'mask_BxSxS2_ik1': mask_BxSxS2_ik1, 'mask_1x1xSxS2_ik1': mask_1x1xSxS2_ik1, 'L0_xattn_Wq': _L0_xattn_in['Wq'], 'L0_xattn_Wk': _L0_xattn_in['Wk'], 'L0_xattn_Wv': _L0_xattn_in['Wv'], 'L0_xattn_Wo': _L0_xattn_in['Wo'], 'L0_ffn_w_gate': _L0_ffn_in['w_gate'], 'L0_ffn_w_up': _L0_ffn_in['w_up'], 'L0_ffn_w_down': _L0_ffn_in['w_down'], 'L1_xattn_Wq': _L1_xattn_in['Wq'], 'L1_xattn_Wk': _L1_xattn_in['Wk'], 'L1_xattn_Wv': _L1_xattn_in['Wv'], 'L1_xattn_Wo': _L1_xattn_in['Wo'], 'L1_xattn_bo': _L1_xattn_in['bo'], 'L1_ffn_W1': _L1_ffn_in['W1'], 'L1_ffn_b1': _L1_ffn_in['b1'], 'L1_ffn_W2': _L1_ffn_in['W2'], 'L1_ffn_b2': _L1_ffn_in['b2'], 'L1_ffn_Wg': _L1_ffn_in['Wg'], 'L1_ffn_bg': _L1_ffn_in['bg']}

def reference(x, ctx_1024, mask_BxSxS2_ik1, mask_1x1xSxS2_ik1, L0_xattn_Wq, L0_xattn_Wk, L0_xattn_Wv, L0_xattn_Wo, L0_ffn_w_gate, L0_ffn_w_up, L0_ffn_w_down, L1_xattn_Wq, L1_xattn_Wk, L1_xattn_Wv, L1_xattn_Wo, L1_xattn_bo, L1_ffn_W1, L1_ffn_b1, L1_ffn_W2, L1_ffn_b2, L1_ffn_Wg, L1_ffn_bg):
    import jax
    import jax.numpy as jnp

    def _L0_xattn_ref(Q, K, V, mask, Wq, Wk, Wv, Wo):
        import jax, jax.numpy as jnp
        import numpy as np
        H = 16
        D_MODEL = 128
        D_K = D_MODEL // H
        NEG = -1000000000.0
        nb, nw, _ = Q.shape
        scaling = jnp.asarray(np.sqrt(D_K), dtype=Q.dtype)
        q = (Q @ Wq.T).reshape(nb, nw, H, D_K).transpose(0, 2, 1, 3)
        k = (K @ Wk.T).reshape(nb, nw, H, D_K).transpose(0, 2, 1, 3)
        v = (V @ Wv.T).reshape(nb, nw, H, D_K).transpose(0, 2, 1, 3)
        scores = jnp.einsum('bhqd,bhkd->bhqk', q, k) / scaling
        scores = jnp.where(mask[:, None, :, :] == 0, jnp.asarray(NEG, scores.dtype), scores)
        probs = jax.nn.softmax(scores, axis=-1)
        attn = jnp.einsum('bhqk,bhkd->bhqd', probs, v)
        x = attn.transpose(0, 2, 1, 3).reshape(nb, nw, D_MODEL)
        return x @ Wo.T

    def _L0_ffn_ref(x, w_gate, w_up, w_down):
        import jax, jax.numpy as jnp
        import numpy as np
        HIDDEN = 128
        INNER = 512

        def _weight_quant(w):
            scale = 1.0 / jnp.clip(jnp.mean(jnp.abs(w)), 1e-05)
            wq = jnp.clip(jnp.round(w * scale), -1.0, 1.0) / scale
            return w + jax.lax.stop_gradient(wq - w)

        def _act_quant(x):
            scale = 127.0 / jnp.clip(jnp.max(jnp.abs(x), axis=-1, keepdims=True), 1e-05)
            xq = jnp.clip(jnp.round(x * scale), -128.0, 127.0) / scale
            return x + jax.lax.stop_gradient(xq - x)

        def _bitlinear(x, w):
            return jnp.einsum('bsi,oi->bso', _act_quant(x), _weight_quant(w))
        gate = jax.nn.silu(_bitlinear(x, w_gate))
        up = _bitlinear(x, w_up)
        return _bitlinear(gate * up, w_down)

    def _L1_xattn_ref(q, k, v, mask, Wq, Wk, Wv, Wo, bo):
        import jax, jax.numpy as jnp
        import numpy as np
        EMBED = 128
        HEADS = 16
        HEAD_DIM = EMBED // HEADS
        B, S = (4, 256)
        N, qlen = (q.shape[0], q.shape[1])
        klen, vlen = (k.shape[1], v.shape[1])
        qh = q.reshape(N, qlen, HEADS, HEAD_DIM)
        kh = k.reshape(N, klen, HEADS, HEAD_DIM)
        vh = v.reshape(N, vlen, HEADS, HEAD_DIM)
        qh = jnp.einsum('nqhd,ed->nqhe', qh, Wq)
        kh = jnp.einsum('nkhd,ed->nkhe', kh, Wk)
        vh = jnp.einsum('nkhd,ed->nkhe', vh, Wv)
        energy = jnp.einsum('nqhd,nkhd->nhqk', qh, kh)
        energy = jnp.where(mask == 0, jnp.float32(-1e+20), energy)
        attention = jax.nn.softmax(energy / jnp.float32(EMBED ** 0.5), axis=3)
        out = jnp.einsum('nhqk,nkhd->nqhd', attention, vh)
        out = out.reshape(N, qlen, EMBED)
        return out @ Wo.T + bo

    def _L1_ffn_ref(x, W1, b1, W2, b2, Wg, bg):
        import jax, jax.numpy as jnp
        import numpy as np
        B, S, D, H, E, K = (4, 128, 128, 256, 8, 2)
        b, s, d = x.shape
        xt = x.reshape(-1, d)
        gate_logits = xt @ Wg.T + bg
        w, idx = jax.lax.top_k(gate_logits, K)
        w = jax.nn.softmax(w, axis=1)
        h = jax.nn.relu(jnp.einsum('td,ehd->eth', xt, W1) + b1[:, None, :])
        y = jnp.einsum('eth,eoh->eto', h, W2) + b2[:, None, :]
        comb = (jax.nn.one_hot(idx, E, dtype=xt.dtype) * w[..., None]).sum(axis=1)
        out = jnp.einsum('eto,te->to', y, comb)
        return out.reshape(b, s, d)
    x = x + _L0_xattn_ref(_layernorm(x, axis=-1), ctx_1024, ctx_1024, mask_BxSxS2_ik1, L0_xattn_Wq, L0_xattn_Wk, L0_xattn_Wv, L0_xattn_Wo)
    x = x + _L0_ffn_ref(_layernorm(x, axis=-1), L0_ffn_w_gate, L0_ffn_w_up, L0_ffn_w_down)
    x = x + _L1_xattn_ref(_layernorm(x, axis=-1), ctx_1024, ctx_1024, mask_1x1xSxS2_ik1, L1_xattn_Wq, L1_xattn_Wk, L1_xattn_Wv, L1_xattn_Wo, L1_xattn_bo)
    x = x + _L1_ffn_ref(_layernorm(x, axis=-1), L1_ffn_W1, L1_ffn_b1, L1_ffn_W2, L1_ffn_b2, L1_ffn_Wg, L1_ffn_bg)
    return x

_drawn_inputs = setup_inputs


def setup_inputs(seed=0):
    import zlib

    import numpy as np

    out = dict(_drawn_inputs(seed))
    spreads = {'L1_ffn_b1': (0.0, 0.648), 'L1_ffn_b2': (0.0, 0.1), 'L1_ffn_bg': (0.0, 0.1)}
    factors = {'L1_xattn_bo': 5.948}
    for name, (base, spread) in spreads.items():
        noise = np.random.default_rng([zlib.crc32(name.encode()), seed]).standard_normal(out[name].shape)
        drawn = base * np.exp(spread * noise) if base else spread * noise
        out[name] = jnp.asarray(drawn.astype(out[name].dtype))
    for name, factor in factors.items():
        out[name] = (out[name] * factor).astype(out[name].dtype)
    return out
```

```python
from contextlib import ExitStack

import concourse.bass as bass
from concourse import mybir

F32 = mybir.dt.float32
BF16 = mybir.dt.bfloat16
I32 = mybir.dt.int32
ALU = mybir.AluOpType
ACT = mybir.ActivationFunctionType
AX = mybir.AxisListType

P = 128
NB = 8
H, DH = 16, 8
UNITS = 2 * NB
GROUPS = H // 2
PAIR = 2 * DH
PARTS = 6
ROWS = PARTS * PAIR
MROWS = ROWS + 6
INNER = 512
E, HID = 8, 256
ZCH = E * HID // P
MASKED = -(2.0 ** 100)
EPS = 1e-5
ROUND = 12582912.0
MAGIC = -554214945.0
QMAX = 127.0
ATTN_SCALE = (DH ** -0.5, P ** -0.5)
SLOTS = UNITS + 6

C_ID, C_SEL, C_W8 = 0, P, P + 2
C_N = P + 2 + E


def timeline():
    order = []
    for t in range(SLOTS):
        p, a, q, s, o = t, t - 1, t - 2, t - 3, t - 4
        f1, f2, m1, m2 = t - 5, t - 6, t - 13, t - 14
        ok = lambda u: 0 <= u < UNITS
        okb = lambda u: 0 <= u < NB
        for beat in range(4):
            if ok(a): order.append(("A", "max", a, beat))
            if ok(s): order.append(("B", "exp", s, beat))
            if beat == 0:
                if ok(p): order.append(("P", "xT", p, 0))
                if ok(o): order.append(("O", "pv", o, 0))
                if okb(m1): order.append(("P", "mxT", m1, 0))
                if okb(f1): order.append(("P", "fxT", f1, 0))
                if okb(m2): order.append(("A", "y", m2, 0))
            if beat == 1:
                if ok(p): order.append(("P", "qkv", p, 0))
                if ok(q): order.append(("Q", "qb", q, 0))
                if ok(o): order.append(("O", "oT", o, 0))
                if okb(f2): order.append(("X", "hT", f2, 0))
                if okb(m1): order.append(("X", "logit", m1, 0))
                if okb(m1): order.append(("B", "z", m1, 0))
                if okb(m2): order.append(("A", "y", m2, 1))
            if beat == 2:
                if ok(o): order.append(("O", "aT", o, 0))
                if ok(p): order.append(("Q", "ks", p, 0))
                if okb(f1): order.append(("A", "gate", f1, 0))
                if okb(f1): order.append(("A", "up", f1, 0))
                if okb(m1): order.append(("B", "z", m1, 1))
            if beat == 3:
                if ok(p): order.append(("Q", "qs", p, 0))
                if ok(o): order.append(("O", "wo", o, 0))
                if okb(f2): order.append(("X", "down", f2, 0))
                if okb(m1): order.append(("B", "z", m1, 2))
                if okb(m1): order.append(("B", "z", m1, 3))
    return order


def build(nc, x, ctxT, mask0, mask0T, mask1, mask1T, w0q, w0kv, w0o, w1q, w1kv, w1o, bo,
          wg, wu, wd, m1T, mb1, m2T, mb2, gT, gb, cst, out):
    order = timeline()
    count, where = {}, {}
    for bank, name, u, i in order:
        where[name, u, i] = (bank, count.get(bank, 0))
        count[bank] = count.get(bank, 0) + 1

    with ExitStack() as ctx:
        def sb(name, shape, dt=F32):
            return ctx.enter_context(nc.sbuf_tensor(name, shape, dt))

        def sem(name):
            return ctx.enter_context(nc.semaphore(name))

        banks = {k: [ctx.enter_context(nc.psum_tensor(f"ps_{k}{i}", [P, 512], F32))
                     for i in range(2 if k in "AB" else 1)] for k in "ABPQOX"}
        full = {k: sem(f"full_{k}") for k in banks}
        free = {k: sem(f"free_{k}") for k in banks}

        def psum(name, u, i=0):
            bank, n = where[name, u, i]
            return banks[bank][n % len(banks[bank])]

        def wait_free(eng, name, u, i=0):
            bank, n = where[name, u, i]
            if n + 1 > len(banks[bank]):
                eng.wait_ge(free[bank], n + 1 - len(banks[bank]))

        def wait_full(eng, name, u, i=0):
            bank, n = where[name, u, i]
            eng.wait_ge(full[bank], n + 1)

        def wait_done(eng, name, u, i=0):
            bank, n = where[name, u, i]
            eng.wait_ge(free[bank], n + 1)

        x_sb = sb("x_sb", [P, NB, P])
        xb_sb = sb("xb_sb", [P, NB, P])
        ctx_sb = sb("ctx_sb", [P, NB, P])
        m0_i = sb("m0_i", [P, NB, P], I32)
        m0T_i = sb("m0T_i", [P, NB, P], I32)
        m1_i = sb("m1_i", [P, P], I32)
        m1T_i = sb("m1T_i", [P, P], I32)
        m0_b = sb("m0_b", [P, NB, P], BF16)
        m0T_b = sb("m0T_b", [P, NB, P], BF16)
        m1_b = sb("m1_b", [P, P], BF16)
        m1T_b = sb("m1T_b", [P, P], BF16)
        wq_sb = [sb(f"wq{l}_sb", [P, P]) for l in range(2)]
        wkv_sb = [sb(f"wkv{l}_sb", [P, 2 * P]) for l in range(2)]
        wo_sb = [sb(f"wo{l}_sb", [P, P]) for l in range(2)]
        bo_sb = sb("bo_sb", [P, P])
        wf_sb = sb("wf_sb", [P, 3, INNER])
        wf_q = sb("wf_q", [P, 3, INNER], BF16)
        wf_t = sb("wf_t", [P, INNER])
        wf_sum = sb("wf_sum", [P, 3])
        wf_mean = sb("wf_mean", [P, 3])
        wf_inv = sb("wf_inv", [P, 3])
        wf_gu = sb("wf_gu", [P, 2])
        w1_sb = sb("w1_sb", [P, ZCH, P])
        w2_sb = sb("w2_sb", [P, ZCH, P])
        b1_sb = sb("b1_sb", [P, ZCH])
        b2_sb = sb("b2_sb", [P, E * P])
        b2_f = sb("b2_f", [P, E * P])
        b2_p = sb("b2_p", [P, 3, E * P], BF16)
        gT_sb = sb("gT_sb", [P, E])
        gb_sb = sb("gb_sb", [P, E])
        cst_sb = sb("cst_sb", [P, C_N])
        id_b = sb("id_b", [P, P], BF16)
        row0 = sb("row0", [P, P], BF16)
        ones = sb("ones", [P, P])
        ident = cst_sb[:, C_ID:C_ID + P]
        w8 = cst_sb[:, C_W8:C_W8 + E]

        st6 = sb("st6", [P, 4, 2, 6])
        mv = sb("mv", [P, 4, 2, 2])
        hv = sb("hv", [P, 4, 2, 1])
        ry = sb("ry", [P, 4, 2, 4])
        rt = sb("rt", [P, 4, 2, 3])
        xh = sb("xh", [P, 4, 2, P])

        xT = sb("xT", [P, 2, P])
        qst = sb("qst", [P, 3, GROUPS, MROWS], BF16)
        kst = sb("kst", [P, 2, GROUPS, MROWS], BF16)
        qr = sb("qr", [P, 2, P])
        kr = sb("kr", [P, 2, P])
        v_sb = sb("v_sb", [P, 5, H, DH + 1])
        qT = sb("qT", [P, 2, GROUPS, P], BF16)
        kT = sb("kT", [P, 5, GROUPS, P], BF16)
        kblk = sb("kblk", [P, 2, GROUPS, 2, P], BF16)
        qblk = sb("qblk", [P, 2, GROUPS, 2, P], BF16)
        mx = sb("mx", [P, 2, H])
        nm = sb("nm", [P, 2, 3, H])
        probs = sb("probs", [P, 2, H, P])
        oT_sb = sb("oT_sb", [P, 2, 4 * P])
        rden = sb("rden", [P, 2, H])
        attn = sb("attn", [P, 2, H, DH])
        aT_sb = sb("aT_sb", [P, 2, P])

        fs = sb("fs", [P, 2, 16])
        xr = sb("xr", [P, 2, P])
        xq = sb("xq", [P, 2, P], BF16)
        xqT = sb("xqT", [P, 2, P], BF16)
        th = sb("th", [P, INNER])
        z1 = sb("z1", [P, INNER])
        z2 = sb("z2", [P, 2, INNER])
        hr = sb("hr", [P, INNER])
        hq = sb("hq", [P, 2, INNER], BF16)
        hqT = sb("hqT", [P, 2, 4, P], BF16)

        mxT = sb("mxT", [P, 2, P])
        lg = sb("lg", [P, 2, 10, E])
        ls = sb("ls", [P, 2, 12])
        comb = sb("comb", [P, 2, E])
        hid = sb("hid", [P, 2, ZCH, P])
        yc = sb("yc", [P, E, P])
        ysum = sb("ysum", [P, 2, P])
        out_sb = sb("out_sb", [P, 2, P])

        s_cst, s_x, s_ctx, s_w0, s_mask, s_w1, s_wf, s_moe = [
            sem(n) for n in ("cst_in", "x_in", "ctx_in", "w0_in", "mask_in", "w1_in", "wf_in", "moe_in")]
        const_ready = sem("const_ready")
        mask_ready = sem("mask_ready")
        wsum_ready, wmean_ready, wq_ready = sem("wsum_ready"), sem("wmean_ready"), sem("wq_ready")
        b2_ready = sem("b2_ready")
        stats_ready = [sem(f"stats_ready{k}") for k in range(4)]
        rstd_ready = [sem(f"rstd_ready{k}") for k in range(4)]
        xh_ready = [sem(f"xh_ready{k}") for k in range(4)]
        xb_ready = sem("xb_ready")
        v_ready, qst_ready, kst_ready, kblk_ready, mpart_ready = [
            sem(n) for n in ("v_ready", "qst_ready", "kst_ready", "kblk_ready", "mpart_ready")]
        c_ready, xq_ready, th_ready, hq_ready = [sem(n) for n in ("c_ready", "xq_ready", "th_ready", "hq_ready")]
        d_ready, e_ready, out_ready = sem("d_ready"), sem("e_ready"), sem("out_ready")
        s_out = [sem("out_stored0"), sem("out_stored1")]
        dve_done, pool_done, act_done = sem("dve_done"), sem("pool_done"), sem("act_done")

        def ln(kind, u):
            return {"attn": 2 * (u // NB), "ffn": 1, "moe": 3}[kind], u % NB

        block = ctx.enter_context(nc.Block())

        @block.sync
        def _(sp):
            sp.dma_start(x_sb[:, 0, :], x[0]).then_inc(s_x, 16)
            sp.dma_start(cst_sb[:, :], cst).then_inc(s_cst, 16)
            sp.dma_start(ctx_sb[:, :, :], ctxT).then_inc(s_ctx, 16)
            sp.dma_start(wq_sb[0][:, :], w0q).then_inc(s_w0, 16)
            sp.dma_start(wkv_sb[0][:, :], w0kv).then_inc(s_w0, 16)
            sp.dma_start(x_sb[:, 1:NB, :], x[1:NB].rearrange("b t d -> t b d")).then_inc(s_x, 16)
            sp.dma_start(m0_i[:, :, :], mask0.rearrange("b q k -> q b k")).then_inc(s_mask, 16)
            sp.dma_start(m0T_i[:, :, :], mask0T).then_inc(s_mask, 16)
            sp.dma_start(m1_i[:, :], mask1).then_inc(s_mask, 16)
            sp.dma_start(m1T_i[:, :], mask1T).then_inc(s_mask, 16)
            sp.dma_start(wo_sb[0][:, :], w0o).then_inc(s_w0, 16)
            sp.dma_start(wf_sb[:, 0, :], wg).then_inc(s_wf, 16)
            sp.dma_start(wf_sb[:, 1, :], wu).then_inc(s_wf, 16)
            sp.dma_start(wf_sb[:, 2, :], wd).then_inc(s_wf, 16)
            for dst, src in ((wq_sb[1], w1q), (wkv_sb[1], w1kv), (wo_sb[1], w1o),
                             (bo_sb, bo.partition_broadcast(P))):
                sp.dma_start(dst[:, :], src).then_inc(s_w1, 16)
            sp.dma_start(w1_sb[:, :, :], m1T).then_inc(s_moe, 16)
            sp.dma_start(w2_sb[:, :, :], m2T).then_inc(s_moe, 16)
            sp.dma_start(b1_sb[:, :], mb1).then_inc(s_moe, 16)
            sp.dma_start(b2_sb[0:1, :], mb2).then_inc(s_moe, 16)
            sp.dma_start(gT_sb[:, :], gT).then_inc(s_moe, 16)
            sp.dma_start(gb_sb[:, :], gb.partition_broadcast(P)).then_inc(s_moe, 16)
            for b in range(NB):
                sp.wait_ge(out_ready, b + 1)
                sp.dma_start(out[b], out_sb[:, b % 2, :]).then_inc(s_out[b % 2], 16)
            for half in s_out:
                sp.wait_ge(half, 8 * NB)

        @block.gpsimd
        def _(pool):
            done = [0]

            def chain(ins):
                done[0] += 1
                ins.then_inc(pool_done, 1)
                pool.wait_ge(pool_done, done[0])

            pool.memset(ones[:, :], 1.0).then_inc(const_ready, 1)
            pool.memset(kst[:, :, :, ROWS:MROWS], 1.0).then_inc(const_ready, 1)
            pool.memset(v_sb[:, :, :, DH:DH + 1], 1.0).then_inc(const_ready, 1)
            pool.memset(row0[:, :], 0.0)
            pool.memset(b2_p[:, :, :], 0.0).then_inc(const_ready, 1)
            pool.wait_ge(const_ready, 4)
            pool.memset(row0[0:1, :], 1.0).then_inc(const_ready, 1)
            pool.wait_ge(s_mask, 64)
            for dst, src in ((m0_b, m0_i), (m0T_b, m0T_i), (m1_b, m1_i), (m1T_b, m1T_i)):
                dst, src = (dst[:, :], src[:, :]) if len(dst.shape) == 2 else (dst[:, :, :], src[:, :, :])
                pool.tensor_scalar(dst, src, 0.0, MASKED, ALU.is_equal, ALU.mult).then_inc(mask_ready, 1)

            def rstd(kind, u):
                k, b = ln(kind, u)
                i = b % 2
                h, y, t = hv[:, k, i, 0:1], ry[:, k, i, :], rt[:, k, i, :]
                pool.wait_ge(stats_ready[k], b + 1)
                chain(pool.tensor_scalar(h, mv[:, k, i, 1:2], EPS, 0.5, ALU.add, ALU.mult))
                chain(pool.tensor_scalar(y[:, 0:1].bitcast(I32), h.bitcast(I32), -0.5, MAGIC, ALU.mult, ALU.add))
                for s in range(3):
                    chain(pool.tensor_scalar(t[:, s:s + 1], y[:, s:s + 1], y[:, s:s + 1], h, ALU.mult, ALU.mult))
                    last = pool.tensor_scalar(y[:, s + 1:s + 2], t[:, s:s + 1], 1.5, y[:, s:s + 1], ALU.subtract, ALU.mult)
                    if s < 2:
                        chain(last)
                last.then_inc(rstd_ready[k], 1)

            for t in range(-1, SLOTS):
                if 0 <= t + 1 < NB:
                    rstd("attn", t + 1)
                if 0 <= t - 4 < NB:
                    rstd("ffn", t - 4)
                if 0 <= t - 12 < NB:
                    rstd("moe", t - 12)
                if 0 <= t - 6 < NB:
                    rstd("attn", t - 6 + NB)
                    b = t - 6
                    if b == 0:
                        pool.wait_ge(s_w1, 64)
                    pool.tensor_tensor(xb_sb[:, b, :], x_sb[:, b, :], bo_sb[:, :], ALU.add).then_inc(xb_ready, 1)

        @block.tensor
        def _(pe):
            def filled(mm, name, u, i=0):
                mm.then_inc(full[where[name, u, i][0]], 1)

            def maxima_scores(n, i):
                l, b = n // NB, n % NB
                o = psum("max", n, i)
                if i == 0:
                    wait_done(pe, "qs", n)
                    pe.wait_ge(kblk_ready, n + 1)
                if n % NB == 0 and i == 0:
                    pe.wait_ge(mask_ready, 4)
                wait_free(pe, "max", n, i)
                m = (m0_b[:, b, :] if l == 0 else m1_b[:, :]).unsqueeze(1).broadcast_to([P, 4, P])
                pe.matmul(o[:, :].rearrange("p (h k) -> p h k", h=4), id_b[:, :], m, start=True, stop=False)
                for g in (2 * i, 2 * i + 1):
                    mm = pe.matmul(o[:, 256 * (g % 2):256 * (g % 2) + 256], qT[0:ROWS, n % 2, g, :],
                                   kblk[0:ROWS, n % 2, g, :, :].rearrange("p a b -> p (a b)"),
                                   start=False, stop=(g % 2 == 1))
                filled(mm, "max", n, i)

            def shifted_scores(n, i):
                l, b = n // NB, n % NB
                o = psum("exp", n, i)
                if i == 0:
                    wait_done(pe, "qb", n)
                wait_free(pe, "exp", n, i)
                m = (m0T_b[:, b, :] if l == 0 else m1T_b[:, :]).unsqueeze(1).broadcast_to([P, 4, P])
                pe.matmul(o[:, :].rearrange("p (h k) -> p h k", h=4), id_b[:, :], m, start=True, stop=False)
                for g in (2 * i, 2 * i + 1):
                    mm = pe.matmul(o[:, 256 * (g % 2):256 * (g % 2) + 256], kT[0:MROWS, n % 5, g, :],
                                   qblk[0:MROWS, n % 2, g, :, :].rearrange("p a b -> p (a b)"),
                                   start=False, stop=(g % 2 == 1))
                filled(mm, "exp", n, i)

            def turn(name, u, src, idn, dt=F32):
                wait_free(pe, name, u)
                o = psum(name, u)
                o = o[:, 0:P] if dt == F32 else o[:, 0:P // 2].bitcast(BF16)
                filled(pe.transpose(o, src, idn), name, u)

            def qkv(n):
                l, b = n // NB, n % NB
                if n == 0:
                    pe.wait_ge(s_w0, 48)
                    pe.wait_ge(s_ctx, 16)
                if n == NB:
                    pe.wait_ge(s_w1, 64)
                wait_free(pe, "qkv", n)
                o = psum("qkv", n)
                pe.matmul(o[:, P:3 * P], ctx_sb[:, b, :], wkv_sb[l][:, :], start=True, stop=True)
                wait_done(pe, "xT", n)
                filled(pe.matmul(o[:, 0:P], xT[:, n % 2, :], wq_sb[l][:, :], start=True, stop=True), "qkv", n)

            def stack(name, n, src, rows):
                wait_free(pe, name, n)
                o = psum(name, n)[:, :].bitcast(BF16)
                for g in range(GROUPS):
                    mm = pe.transpose(o[0:rows, g * P:(g + 1) * P], src[:, g, 0:rows], id_b[:, :])
                filled(mm, name, n)

            def weighted_values(n):
                wait_free(pe, "pv", n)
                pe.wait_ge(v_ready, n + 1)
                wait_done(pe, "exp", n, 3)
                o = psum("pv", n)
                for h in range(H):
                    j = h % 4
                    mm = pe.matmul(o[32 * j:32 * j + DH + 1, (h // 4) * P:(h // 4 + 1) * P], v_sb[:, n % 5, h, :],
                                   probs[:, n % 2, h, :], start=True, stop=True)
                filled(mm, "pv", n)

            def turn_outputs(n):
                wait_free(pe, "oT", n)
                wait_done(pe, "pv", n)
                o = psum("oT", n)
                for g in range(4):
                    mm = pe.transpose(o[:, g * P:(g + 1) * P], oT_sb[:, n % 2, g * P:(g + 1) * P], ident)
                filled(mm, "oT", n)

            def project(n):
                wait_free(pe, "wo", n)
                wait_done(pe, "aT", n)
                filled(pe.matmul(psum("wo", n)[:, 0:P], aT_sb[:, n % 2, :], wo_sb[n // NB][:, :],
                                 start=True, stop=True), "wo", n)

            def gate_up(b):
                if b == 0:
                    pe.wait_ge(wq_ready, 3)
                wait_done(pe, "fxT", b)
                for k, name in enumerate(("gate", "up")):
                    wait_free(pe, name, b)
                    filled(pe.matmul(psum(name, b)[:, :], xqT[:, b % 2, :], wf_q[:, k, :], start=True, stop=True), name, b)

            def turn_hidden(b):
                wait_free(pe, "hT", b)
                pe.wait_ge(hq_ready, b + 1)
                o = psum("hT", b)[:, 0:256].bitcast(BF16)
                for c in range(4):
                    mm = pe.transpose(o[:, c * P:(c + 1) * P], hq[:, b % 2, c * P:(c + 1) * P], id_b[:, :])
                filled(mm, "hT", b)

            def down(b):
                wait_free(pe, "down", b)
                wait_done(pe, "hT", b)
                for c in range(4):
                    mm = pe.matmul(psum("down", b)[:, 0:P], hqT[:, b % 2, c, :], wf_q[:, 2, c * P:(c + 1) * P],
                                   start=(c == 0), stop=(c == 3))
                filled(mm, "down", b)

            def logits(b):
                if b == 0:
                    pe.wait_ge(s_moe, 96)
                wait_free(pe, "logit", b)
                wait_done(pe, "mxT", b)
                filled(pe.matmul(psum("logit", b)[:, 0:E], mxT[:, b % 2, :], gT_sb[:, :], start=True, stop=True), "logit", b)

            def hidden(b, i):
                wait_free(pe, "z", b, i)
                for c in range(4):
                    mm = pe.matmul(psum("z", b, i)[:, c * P:(c + 1) * P], w1_sb[:, 4 * i + c, :], mxT[:, b % 2, :],
                                   start=True, stop=True)
                filled(mm, "z", b, i)

            def experts(b, i):
                if b == 0 and i == 0:
                    pe.wait_ge(b2_ready, 1)
                    pe.wait_ge(const_ready, 5)
                wait_free(pe, "y", b, i)
                o = psum("y", b, i)
                for part in range(3):
                    pe.matmul(o[:, :], row0[:, :], b2_p[:, part, i * 512:(i + 1) * 512], start=(part == 0), stop=False)
                wait_done(pe, "z", b, 2 * i + 1)
                for c in range(8 * i, 8 * i + 8):
                    e = c // 2 - 4 * i
                    mm = pe.matmul(o[:, e * P:(e + 1) * P], hid[:, b % 2, c, :], w2_sb[:, c, :],
                                   start=False, stop=(c == 8 * i + 7))
                filled(mm, "y", b, i)

            pe.wait_ge(s_cst, 16)
            pe.wait_ge(dve_done, 1)
            for bank, name, u, i in order:
                if name == "max": maxima_scores(u, i)
                if name == "exp": shifted_scores(u, i)
                if name == "xT":
                    k, b = ln("attn", u)
                    pe.wait_ge(xh_ready[k], b + 1)
                    turn("xT", u, xh[:, k, b % 2, :], ident)
                if name == "fxT":
                    pe.wait_ge(xq_ready, u + 1)
                    turn("fxT", u, xq[:, u % 2, :], id_b[:, :], BF16)
                if name == "mxT":
                    pe.wait_ge(xh_ready[3], u + 1)
                    turn("mxT", u, xh[:, 3, u % 2, :], ident)
                if name == "qkv": qkv(u)
                if name == "ks":
                    pe.wait_ge(kst_ready, u + 1)
                    stack("ks", u, kst[:, u % 2, :, :], MROWS)
                if name == "qs":
                    pe.wait_ge(qst_ready, u + 1)
                    stack("qs", u, qst[:, u % 3, :, :], ROWS)
                if name == "qb":
                    pe.wait_ge(mpart_ready, u + 1)
                    stack("qb", u, qst[:, u % 3, :, :], MROWS)
                if name == "pv": weighted_values(u)
                if name == "oT": turn_outputs(u)
                if name == "aT":
                    wait_done(pe, "oT", u)
                    turn("aT", u, attn[:, u % 2, :, :].rearrange("p h d -> p (h d)"), ident)
                if name == "wo": project(u)
                if name == "gate": gate_up(u)
                if name == "hT": turn_hidden(u)
                if name == "down": down(u)
                if name == "logit": logits(u)
                if name == "z": hidden(u, i)
                if name == "y": experts(u, i)
                if name == "qkv" and u == 0:
                    pe.wait_ge(wsum_ready, 3)
                    pe.wait_ge(const_ready, 5)
                    pe.wait_ge(dve_done, 2)
                    pe.matmul(banks["X"][0][:, 0:3], ones[:, :], wf_sum[:, :], start=True, stop=True).then_inc(wmean_ready, 1)

        @block.scalar
        def _(act):
            def freed(ins, name, u, i=0):
                ins.then_inc(free[where[name, u, i][0]], 1)

            def evacuate(dst, name, u, src):
                wait_full(act, name, u)
                ins = act.activation(dst, src, ACT.Copy)
                freed(ins, name, u)

            def high_parts(n):
                wait_full(act, "qkv", n)
                o = psum("qkv", n)
                if n >= 3:
                    act.wait_ge(full["Q"], where["qb", n - 3, 0][1] + 1)
                if n >= 2:
                    act.wait_ge(full["Q"], where["ks", n - 2, 0][1] + 1)
                if n == 0:
                    act.wait_ge(const_ready, 5)
                grp = lambda ap: ap.rearrange("p (g r) -> p g r", g=GROUPS)
                for c in range(3):
                    act.activation(qst[:, n % 3, :, (3 + c) * PAIR:(4 + c) * PAIR], grp(o[:, 0:P]), ACT.Copy)
                for c in range(3):
                    act.activation(kst[:, n % 2, :, (1 + c) * PAIR:(2 + c) * PAIR], grp(o[:, P:2 * P]), ACT.Copy)
                if n >= 5:
                    act.wait_ge(full["O"], where["pv", n - 5, 0][1] + 1)
                act.activation(v_sb[:, n % 5, :, 0:DH], o[:, 2 * P:3 * P].rearrange("p (h d) -> p h d", h=H),
                               ACT.Copy).then_inc(v_ready, 1)

            def exps(n, i):
                wait_full(act, "exp", n, i)
                if n >= 2 and i == 0:
                    act.wait_ge(full["O"], where["pv", n - 2, 0][1] + 1)
                ins = act.activation(probs[:, n % 2, 4 * i:4 * i + 4, :],
                                     psum("exp", n, i)[:, :].rearrange("p (h k) -> p h k", h=4),
                                     ACT.Exp, scale=ATTN_SCALE[n // NB])
                freed(ins, "exp", n, i)

            def relu(b, i):
                wait_full(act, "z", b, i)
                if b >= 2 and i == 0:
                    act.wait_ge(full["A"], where["y", b - 2, 1][1] + 1)
                for c in range(4):
                    ins = act.activation(hid[:, b % 2, 4 * i + c, :], psum("z", b, i)[:, c * P:(c + 1) * P],
                                         ACT.Relu, bias=b1_sb[:, 4 * i + c:4 * i + c + 1])
                freed(ins, "z", b, i)

            for bank, name, u, i in order:
                if name == "exp": exps(u, i)
                if name == "xT":
                    if u >= 2:
                        act.wait_ge(full["P"], where["qkv", u - 2, 0][1] + 1)
                    evacuate(xT[:, u % 2, :], "xT", u, psum("xT", u)[:, 0:P])
                if name == "fxT":
                    if u >= 2:
                        act.wait_ge(full["A"], where["up", u - 2, 0][1] + 1)
                    evacuate(xqT[:, u % 2, :], "fxT", u, psum("fxT", u)[:, 0:P // 2].bitcast(BF16))
                if name == "mxT":
                    if u >= 2:
                        act.wait_ge(full["B"], where["z", u - 2, 3][1] + 1)
                    evacuate(mxT[:, u % 2, :], "mxT", u, psum("mxT", u)[:, 0:P])
                if name == "qkv": high_parts(u)
                if name == "ks":
                    if u >= 5:
                        act.wait_ge(full["B"], where["exp", u - 5, 3][1] + 1)
                    evacuate(kT[0:MROWS, u % 5, :, :].rearrange("p g k -> p (g k)"), "ks", u,
                             psum("ks", u)[0:MROWS, :].bitcast(BF16))
                if name == "pv":
                    if u >= 2:
                        act.wait_ge(full["O"], where["oT", u - 2, 0][1] + 1)
                    if u == 0:
                        act.wait_ge(const_ready, 5)
                    evacuate(oT_sb[:, u % 2, :], "pv", u, psum("pv", u)[:, :])
                if name == "aT":
                    if u >= 2:
                        act.wait_ge(full["O"], where["wo", u - 2, 0][1] + 1)
                    evacuate(aT_sb[:, u % 2, :], "aT", u, psum("aT", u)[:, 0:P])
                if name == "up":
                    wait_full(act, "gate", u)
                    act.wait_ge(c_ready, u + 1)
                    if u >= 1:
                        wait_done(act, "up", u - 1)
                    act.activation(th[:, :], psum("gate", u)[:, :], ACT.Tanh, scale=fs[:, u % 2, 4:5]).then_inc(th_ready, 1)
                if name == "hT":
                    if u >= 2:
                        act.wait_ge(full["X"], where["down", u - 2, 0][1] + 1)
                    evacuate(hqT[:, u % 2, :, :].rearrange("p c t -> p (c t)"), "hT", u,
                             psum("hT", u)[:, 0:256].bitcast(BF16))
                if name == "z": relu(u, i)
                if name == "logit":
                    act.wait_ge(d_ready, u + 1)
                    act.activation(ls[:, u % 2, 5:6], ls[:, u % 2, 4:5], ACT.Exp).then_inc(e_ready, 1)

        @block.vector
        def _(dve):
            done = [0]

            def mark(ins):
                done[0] += 1
                ins.then_inc(dve_done, 1)
                return done[0]

            def chain(ins):
                dve.wait_ge(dve_done, mark(ins))

            def freed(ins, name, u, i=0):
                ins.then_inc(free[where[name, u, i][0]], 1)

            def stats(kind, u):
                k, b = ln(kind, u)
                if u == 0 or (k == 0 and b == 1):
                    dve.wait_ge(s_x, 16 if b == 0 else 32)
                chain(dve.bn_stats(st6[:, k, b % 2, :], x_sb[:, b, :]))
                dve.bn_aggr(mv[:, k, b % 2, :], st6[:, k, b % 2, :]).then_inc(stats_ready[k], 1)

            def normalise(kind, u):
                k, b = ln(kind, u)
                dve.wait_ge(rstd_ready[k], b + 1)
                if b >= 2:
                    if k in (0, 2):
                        dve.wait_ge(full["P"], where["xT", u - 2, 0][1] + 1)
                    if k == 3:
                        dve.wait_ge(full["P"], where["mxT", u - 2, 0][1] + 1)
                ins = dve.tensor_scalar(xh[:, k, b % 2, :], x_sb[:, b, :], mv[:, k, b % 2, 0:1], ry[:, k, b % 2, 3:4],
                                        ALU.subtract, ALU.mult)
                ins.then_inc(xh_ready[k], 1)

            def low_parts(n):
                o = psum("qkv", n)
                grp = lambda ap: ap.rearrange("p (g r) -> p g r", g=GROUPS)
                dve.wait_ge(v_ready, n + 1)
                st, i = qst[:, n % 3, :, :], n % 2
                dve.tensor_tensor(grp(qr[:, i, :]), grp(o[:, 0:P]), st[:, :, 3 * PAIR:4 * PAIR], ALU.subtract)
                kk = kst[:, i, :, :]
                ins = dve.tensor_tensor(grp(kr[:, i, :]), grp(o[:, P:2 * P]), kk[:, :, PAIR:2 * PAIR], ALU.subtract)
                freed(ins, "qkv", n)
                wait_done(dve, "qkv", n)
                two = lambda ap: ap.rearrange("p (g a r) -> p g a r", g=GROUPS, a=1).broadcast_to([P, GROUPS, 2, PAIR])
                dve.tensor_copy(st[:, :, 0:2 * PAIR].rearrange("p g (c r) -> p g c r", c=2), two(qr[:, i, :]))
                dve.tensor_copy(kk[:, :, 0:PAIR], grp(kr[:, i, :]))
                chain(dve.tensor_copy(kk[:, :, 4 * PAIR:5 * PAIR], grp(kr[:, i, :])))
                dve.tensor_tensor(st[:, :, 2 * PAIR:3 * PAIR], grp(qr[:, i, :]), st[:, :, 0:PAIR],
                                  ALU.subtract).then_inc(qst_ready, 1)
                dve.tensor_tensor(kk[:, :, 5 * PAIR:6 * PAIR], grp(kr[:, i, :]), kk[:, :, 0:PAIR],
                                  ALU.subtract).then_inc(kst_ready, 1)

            def key_blocks(n):
                wait_done(dve, "ks", n)
                if n >= 2:
                    dve.wait_ge(full["A"], where["max", n - 2, 3][1] + 1)
                for j in range(2):
                    ins = dve.tensor_scalar(kblk[0:ROWS, n % 2, :, j, :], kT[0:ROWS, n % 5, :, :],
                                            cst_sb[0:ROWS, C_SEL + j:C_SEL + j + 1], None, ALU.mult)
                ins.then_inc(kblk_ready, 1)

            def query_blocks(n):
                wait_full(dve, "qb", n)
                if n >= 2:
                    dve.wait_ge(full["B"], where["exp", n - 2, 3][1] + 1)
                src = psum("qb", n)[0:MROWS, :].bitcast(BF16).rearrange("p (g k) -> p g k", g=GROUPS)
                for j in range(2):
                    ins = dve.tensor_scalar(qblk[0:MROWS, n % 2, :, j, :], src,
                                            cst_sb[0:MROWS, C_SEL + j:C_SEL + j + 1], None, ALU.mult)
                freed(ins, "qb", n)

            def query_stack(n):
                wait_full(dve, "qs", n)
                if n >= 2:
                    dve.wait_ge(full["A"], where["max", n - 2, 3][1] + 1)
                ins = dve.tensor_copy(qT[0:ROWS, n % 2, :, :].rearrange("p g k -> p (g k)"),
                                      psum("qs", n)[0:ROWS, :].bitcast(BF16))
                freed(ins, "qs", n)

            def maxima(n, i):
                wait_full(dve, "max", n, i)
                ins = dve.tensor_reduce(mx[:, n % 2, 4 * i:4 * i + 4],
                                        psum("max", n, i)[:, :].rearrange("p (h k) -> p h k", h=4), AX.X, ALU.max)
                freed(ins, "max", n, i)

            def maxima_parts(n):
                i = n % 2
                st = qst[:, n % 3, :, ROWS:MROWS].rearrange("p g (j c) -> p g j c", j=2)
                hd = lambda ap: ap.rearrange("p (g j) -> p g j", j=2)
                m = [hd(nm[:, i, c, :]) for c in range(3)]
                chain(dve.tensor_scalar(nm[:, i, 0, :], mx[:, i, :], -1.0, None, ALU.mult))
                chain(dve.tensor_copy(st[:, :, :, 0], m[0]))
                chain(dve.tensor_tensor(m[1], m[0], st[:, :, :, 0], ALU.subtract))
                chain(dve.tensor_copy(st[:, :, :, 1], m[1]))
                dve.tensor_tensor(st[:, :, :, 2], m[1], st[:, :, :, 1], ALU.subtract).then_inc(mpart_ready, 1)

            def divide(n):
                wait_full(dve, "oT", n)
                o = psum("oT", n)[:, :].rearrange("p (h r) -> p h r", h=H)
                i = n % 2
                chain(dve.reciprocal(rden[:, i, :].unsqueeze(2), o[:, :, DH:DH + 1]))
                if n >= 2:
                    dve.wait_ge(full["O"], where["aT", n - 2, 0][1] + 1)
                ins = dve.tensor_tensor(attn[:, i, :, :], o[:, :, 0:DH],
                                        rden[:, i, :].unsqueeze(2).broadcast_to([P, H, DH]), ALU.mult)
                freed(ins, "oT", n)

            def add_attention(n):
                b = n % NB
                wait_full(dve, "wo", n)
                if n >= NB:
                    dve.wait_ge(xb_ready, b + 1)
                res = x_sb[:, b, :] if n < NB else xb_sb[:, b, :]
                ins = dve.tensor_tensor(x_sb[:, b, :], psum("wo", n)[:, 0:P], res, ALU.add)
                freed(ins, "wo", n)
                wait_done(dve, "wo", n)

            def quantise_x(b):
                i = b % 2
                f = lambda c: fs[:, i, c:c + 1]
                dve.wait_ge(xh_ready[1], b + 1)
                chain(dve.tensor_reduce(f(0), xh[:, 1, i, :], AX.X, ALU.max, apply_absolute_value=True))
                chain(dve.tensor_scalar(f(1), f(0), EPS, None, ALU.max))
                if b == 0:
                    dve.wait_ge(wq_ready, 3)
                dve.tensor_scalar(f(4), f(1), wf_gu[:, 0:1], None, ALU.mult).then_inc(c_ready, 1)
                dve.tensor_scalar(f(5), f(1), f(1), wf_gu[:, 1:2], ALU.mult, ALU.mult)
                chain(dve.reciprocal(f(2), f(1)))
                chain(dve.tensor_scalar(f(3), f(2), QMAX, None, ALU.mult))
                chain(dve.tensor_scalar(xr[:, i, :], xh[:, 1, i, :], f(3), ROUND, ALU.mult, ALU.add))
                if b >= 2:
                    dve.wait_ge(full["P"], where["fxT", b - 2, 0][1] + 1)
                dve.tensor_scalar(xq[:, i, :], xr[:, i, :], ROUND, QMAX, ALU.subtract, ALU.min).then_inc(xq_ready, 1)

            def gate_times_up(b):
                dve.wait_ge(th_ready, b + 1)
                ins = dve.scalar_tensor_tensor(out=z1[:, :], in0=th[:, :], scalar=1.0, in1=psum("gate", b)[:, :],
                                               op0=ALU.add, op1=ALU.mult)
                freed(ins, "gate", b)
                wait_done(dve, "gate", b)
                wait_full(dve, "up", b)
                ins = dve.tensor_tensor(z2[:, b % 2, :], z1[:, :], psum("up", b)[:, :], ALU.mult)
                freed(ins, "up", b)

            def quantise_h(b):
                i = b % 2
                f = lambda c: fs[:, i, c:c + 1]
                wait_done(dve, "up", b)
                chain(dve.tensor_reduce(f(7), z2[:, i, :], AX.X, ALU.max, apply_absolute_value=True))
                chain(dve.tensor_scalar(f(8), f(7), f(5), EPS, ALU.mult, ALU.max))
                dve.tensor_scalar(f(13), f(8), wf_mean[:, 2:3], 1.0 / QMAX, ALU.mult, ALU.mult)
                chain(dve.reciprocal(f(10), f(8)))
                chain(dve.tensor_scalar(f(11), f(10), QMAX, f(5), ALU.mult, ALU.mult))
                chain(dve.tensor_scalar(hr[:, :], z2[:, i, :], f(11), ROUND, ALU.mult, ALU.add))
                if b >= 2:
                    dve.wait_ge(full["X"], where["hT", b - 2, 0][1] + 1)
                dve.tensor_scalar(hq[:, i, :], hr[:, :], ROUND, QMAX, ALU.subtract, ALU.min).then_inc(hq_ready, 1)

            def add_ffn(b):
                wait_full(dve, "down", b)
                ins = dve.scalar_tensor_tensor(out=x_sb[:, b, :], in0=psum("down", b)[:, 0:P], scalar=fs[:, b % 2, 13:14],
                                               in1=x_sb[:, b, :], op0=ALU.mult, op1=ALU.add)
                freed(ins, "down", b)
                wait_done(dve, "down", b)

            def top2(b):
                i = b % 2
                L = lambda c: lg[:, i, c, :]
                s = lambda c: ls[:, i, c:c + 1]
                wait_full(dve, "logit", b)
                if b == 0:
                    dve.wait_ge(s_moe, 96)
                ins = dve.tensor_tensor(L(0), psum("logit", b)[:, 0:E], gb_sb[:, :], ALU.add)
                freed(ins, "logit", b)
                wait_done(dve, "logit", b)
                for r in range(2):
                    v, key, hot = s(2 * r), s(2 * r + 1), L(3 * r + 2)
                    chain(dve.tensor_reduce(v, L(3 * r), AX.X, ALU.max))
                    chain(dve.scalar_tensor_tensor(out=L(3 * r + 1), in0=L(3 * r), scalar=v, in1=w8,
                                                   op0=ALU.is_ge, op1=ALU.mult))
                    chain(dve.tensor_reduce(key, L(3 * r + 1), AX.X, ALU.max))
                    chain(dve.tensor_scalar(hot, w8, key, None, ALU.is_equal))
                    if r == 0:
                        chain(dve.scalar_tensor_tensor(out=L(3), in0=hot, scalar=-3.0e38, in1=L(0),
                                                       op0=ALU.mult, op1=ALU.add))
                dve.tensor_scalar(s(4), s(2), s(0), None, ALU.subtract).then_inc(d_ready, 1)

            def combine(b):
                i = b % 2
                L = lambda c: lg[:, i, c, :]
                s = lambda c: ls[:, i, c:c + 1]
                dve.wait_ge(e_ready, b + 1)
                chain(dve.tensor_scalar(s(6), s(5), 1.0, None, ALU.add))
                chain(dve.reciprocal(s(7), s(6)))
                chain(dve.tensor_scalar(s(8), s(5), s(7), None, ALU.mult))
                chain(dve.tensor_scalar(L(8), L(2), s(7), None, ALU.mult))
                chain(dve.scalar_tensor_tensor(out=comb[:, i, :], in0=L(5), scalar=s(8), in1=L(8),
                                               op0=ALU.mult, op1=ALU.add))

            def weigh(b, i):
                wait_full(dve, "y", b, i)
                ins = dve.tensor_tensor(yc[:, 4 * i:4 * i + 4, :], psum("y", b, i)[:, :].rearrange("p (e o) -> p e o", e=4),
                                        comb[:, b % 2, 4 * i:4 * i + 4].unsqueeze(2).broadcast_to([P, 4, P]), ALU.mult)
                freed(ins, "y", b, i)
                if i == 0:
                    return
                wait_done(dve, "y", b, i)
                chain(dve.tensor_reduce(ysum[:, b % 2, :], yc[:, :, :].rearrange("p e o -> p o e"), AX.X, ALU.add))
                if b >= 2:
                    dve.wait_ge(s_out[b % 2], 16 * (b // 2))
                dve.tensor_tensor(out_sb[:, b % 2, :], ysum[:, b % 2, :], x_sb[:, b, :], ALU.add).then_inc(out_ready, 1)

            def ternary_weights():
                dve.wait_ge(wmean_ready, 1)
                chain(dve.tensor_scalar(wf_mean[:, :], banks["X"][0][:, 0:3], 1.0 / (P * INNER), EPS, ALU.mult, ALU.max))
                chain(dve.reciprocal(wf_inv[:, :], wf_mean[:, :]))
                dve.tensor_scalar(wf_gu[:, 0:1], wf_mean[:, 0:1], 0.5 / QMAX, None, ALU.mult)
                chain(dve.tensor_scalar(wf_gu[:, 1:2], wf_mean[:, 0:1], wf_mean[:, 1:2], 0.5 / QMAX / QMAX, ALU.mult, ALU.mult))
                for k in range(3):
                    if k:
                        dve.wait_ge(wq_ready, k)
                    chain(dve.tensor_scalar(wf_t[:, :], wf_sb[:, k, :], wf_inv[:, k:k + 1], ROUND, ALU.mult, ALU.add))
                    chain(dve.tensor_scalar(wf_t[:, :], wf_t[:, :], ROUND, 1.0, ALU.subtract, ALU.min))
                    dve.tensor_scalar(wf_q[:, k, :], wf_t[:, :], -1.0, None, ALU.max).then_inc(wq_ready, 1)

            def bias_parts():
                dve.wait_ge(s_moe, 96)
                dve.wait_ge(const_ready, 5)
                chain(dve.tensor_copy(b2_p[0:1, 0, :], b2_sb[0:1, :]))
                chain(dve.tensor_tensor(b2_f[0:1, :], b2_sb[0:1, :], b2_p[0:1, 0, :], ALU.subtract))
                chain(dve.tensor_copy(b2_p[0:1, 1, :], b2_f[0:1, :]))
                dve.tensor_tensor(b2_p[0:1, 2, :], b2_f[0:1, :], b2_p[0:1, 1, :], ALU.subtract).then_inc(b2_ready, 1)

            dve.wait_ge(s_cst, 16)
            mark(dve.tensor_copy(id_b[:, :], ident))
            mark(dve.memset(banks["O"][0][:, :], 0.0))
            stats("attn", 0)
            dve.wait_ge(s_wf, 48)
            for k in range(3):
                dve.tensor_reduce(wf_sum[:, k:k + 1], wf_sb[:, k, :], AX.X, ALU.add,
                                  apply_absolute_value=True).then_inc(wsum_ready, 1)
            normalise("attn", 0)
            for bank, name, u, i in order:
                if name == "max":
                    maxima(u, i)
                    if i == 3:
                        wait_done(dve, "max", u, 3)
                        maxima_parts(u)
                if name == "xT" and u + 1 < NB:
                    stats("attn", u + 1)
                if name == "qkv":
                    low_parts(u)
                    if u == 0:
                        ternary_weights()
                    if u == 1:
                        bias_parts()
                    if u + 1 < NB:
                        normalise("attn", u + 1)
                if name == "ks": key_blocks(u)
                if name == "qs": query_stack(u)
                if name == "qb": query_blocks(u)
                if name == "oT": divide(u)
                if name == "wo":
                    add_attention(u)
                    kind = "ffn" if u < NB else "moe"
                    stats(kind, u % NB)
                    normalise(kind, u % NB)
                    if u < NB:
                        quantise_x(u)
                if name == "up":
                    gate_times_up(u)
                    quantise_h(u)
                if name == "down":
                    add_ffn(u)
                    stats("attn", NB + u)
                    normalise("attn", NB + u)
                if name == "logit":
                    top2(u)
                    combine(u)
                if name == "y": weigh(u, i)


_ORDER = ["x", "ctxT", "mask0", "mask0T", "mask1", "mask1T", "w0q", "w0kv", "w0o", "w1q", "w1kv", "w1o", "bo",
          "wg", "wu", "wd", "m1T", "mb1", "m2T", "mb2", "gT", "gb", "cst"]


def kernel(**inputs):
    import numpy as np
    import concourse.bacc as bacc
    from concourse.bass_utils import run_bass_kernel_spmd

    a = {k: np.asarray(v) for k, v in inputs.items()}

    def per_head(w):
        big = np.zeros((P, P), w.dtype)
        for h in range(H):
            big[h * DH:(h + 1) * DH, h * DH:(h + 1) * DH] = w.T
        return big

    cst = np.zeros((P, C_N), np.float32)
    cst[:, C_ID:C_ID + P] = np.eye(P)
    for r in range(MROWS):
        cst[r, C_SEL + ((r % PAIR) // DH if r < ROWS else (r - ROWS) // 3)] = 1.0
    cst[:, C_W8:C_W8 + E] = np.arange(E, 0, -1)
    data = {
        "x": a["x"],
        "ctxT": a["ctx_1024"].transpose(2, 0, 1),
        "mask0": a["mask_BxSxS2_ik1"],
        "mask0T": a["mask_BxSxS2_ik1"].transpose(2, 0, 1),
        "mask1": a["mask_1x1xSxS2_ik1"][0, 0],
        "mask1T": a["mask_1x1xSxS2_ik1"][0, 0].T,
        "w0q": a["L0_xattn_Wq"].T,
        "w0kv": np.concatenate([a["L0_xattn_Wk"].T, a["L0_xattn_Wv"].T], axis=1),
        "w0o": a["L0_xattn_Wo"].T,
        "w1q": per_head(a["L1_xattn_Wq"]),
        "w1kv": np.concatenate([per_head(a["L1_xattn_Wk"]), per_head(a["L1_xattn_Wv"])], axis=1),
        "w1o": a["L1_xattn_Wo"].T,
        "bo": a["L1_xattn_bo"],
        "wg": a["L0_ffn_w_gate"].T,
        "wu": a["L0_ffn_w_up"].T,
        "wd": a["L0_ffn_w_down"].T.reshape(INNER // P, P, P).transpose(1, 0, 2).reshape(P, INNER),
        "m1T": a["L1_ffn_W1"].reshape(ZCH, P, P).transpose(2, 0, 1),
        "mb1": a["L1_ffn_b1"].reshape(ZCH, P).T,
        "m2T": a["L1_ffn_W2"].transpose(0, 2, 1).reshape(ZCH, P, P).transpose(1, 0, 2),
        "mb2": a["L1_ffn_b2"].reshape(1, E * P),
        "gT": a["L1_ffn_Wg"].T,
        "gb": a["L1_ffn_bg"],
        "cst": cst,
    }
    nc = bacc.Bacc("TRN2", target_bir_lowering=False, num_devices=1)
    arrays, args = {}, []
    for name in _ORDER:
        v = np.ascontiguousarray(data[name])
        arrays[f"in_{name}"] = v
        args.append(nc.dram_tensor(f"in_{name}", v.shape, mybir.dt.from_np(v.dtype), kind="ExternalInput").ap())
    args.append(nc.dram_tensor("out_y", (NB, P, P), F32, kind="ExternalOutput").ap())
    build(nc, *args)
    r = run_bass_kernel_spmd(nc, [arrays], core_ids=[0])
    return r.results[0]["out_y"]
```

```python
from contextlib import ExitStack

import concourse.bass as bass
from concourse import mybir

F32 = mybir.dt.float32
BF16 = mybir.dt.bfloat16
I32 = mybir.dt.int32
ALU = mybir.AluOpType
ACT = mybir.ActivationFunctionType
AX = mybir.AxisListType

P = 128
NB = 8
H, DH = 16, 8
UNITS = 2 * NB
GROUPS = H // 2
PAIR = 2 * DH
PARTS = 6
ROWS = PARTS * PAIR
MROWS = ROWS + 6
INNER = 512
E, HID = 8, 256
ZCH = E * HID // P
MASKED = -(2.0 ** 100)
EPS = 1e-5
ROUND = 12582912.0
MAGIC = -554214945.0
QMAX = 127.0
ATTN_SCALE = (DH ** -0.5, P ** -0.5)

BANK = {"max": "A", "gate": "B", "up": "A", "y": "A", "exp": "B", "z": "B", "xT": "P", "qkv": "P", "fxT": "P",
        "mxT": "P", "qb": "Q", "ks": "Q", "qs": "Q", "pv": "O", "oT": "O", "aT": "O", "wo": "O",
        "hT": "X", "down": "X", "logit": "X"}
PER_BATCH = ("fxT", "gate", "up", "hT", "down", "mxT", "logit", "z", "y")

C_ID, C_SEL, C_W8, C_R12, C_R2 = 0, P, P + 2, P + 2 + E, P + 3 + E
C_N = P + 4 + E


START = (13, 18.6)
PE_AT = (
    {"xT": -1.2, "qkv": 1.7, "ks": 7.1, "qs": 8.4, "max": (12, 13.1, 14.1, 15.2), "qb": 26.3,
     "exp": (28.7, 29.6, 30.5, 31.4), "pv": 37.8, "oT": 39.5, "aT": 44.4, "wo": 45.2, "fxT": 52.7, "gate": 53,
     "up": 53.9, "hT": 60.1, "down": 61.3},
    {"xT": -2, "qkv": 2, "ks": 6.7, "qs": 8.5, "max": (12.2, 13.4, 14.6, 15.8), "qb": 18.9,
     "exp": (24.4, 25.1, 25.9, 26.6), "pv": 31.9, "oT": 34, "aT": 36.8, "wo": 37.7, "mxT": 52, "logit": 55.3,
     "z": (54.2, 55.7, 57.2, 58.7), "y": (61.1, 65)},
)
DVE_LAG, ACT_LAG = 1, 2.5
DVE_AT = (
    {"stats": -11, "norm": -5.3, "kblk": 9.3, "parts": 21.7, "fnorm": 49.5, "qx": 51.2, "z1": 54, "qh": 58.5},
    {"norm": -5.7, "kblk": 9.1, "parts": 17.9, "fnorm": 40.3, "top": 56.3, "comb": 60.4},
)
ACT_AT = (
    {},
    {"e": 62.6},
)

POOL_AT = (
    {"rstd": -6.5, "masks": 9.3, "frstd": 46},
    {"rstd": -37.9, "masks": -4.1, "frstd": 37, "sum": 69.4},
)


def timeline(at, lag=0.0, extra=None):
    steps = []
    for n in range(UNITS):
        layer = n // NB
        start = n * START[0] if layer == 0 else NB * START[0] + (n - NB) * START[1]
        for name, when in at[layer].items():
            for i, w in enumerate(when if isinstance(when, tuple) else (when,)):
                steps.append((start + w + lag, name, n, i))
        for name, when in (extra[layer] if extra else {}).items():
            steps.append((start + when, name, n, 0))
    return [s[1:] for s in sorted(steps)]


def build(nc, x, ctxT, mask0, mask0T, mask1, mask1T, w0q, w0kv, w0o, w1q, w1kv, w1o, bo,
          wg, wu, wd, m1T, mb1, m2T, mb2, gT, gb, cst, out):
    count, where = {}, {}
    for name, n, i in timeline(PE_AT):
        bank = BANK[name]
        u = n % NB if name in PER_BATCH else n
        where[name, u, i] = (bank, count.get(bank, 0))
        count[bank] = count.get(bank, 0) + 1

    with ExitStack() as ctx:
        def sb(name, shape, dt=F32):
            return ctx.enter_context(nc.sbuf_tensor(name, shape, dt))

        def sem(name):
            return ctx.enter_context(nc.semaphore(name))

        banks = {k: [ctx.enter_context(nc.psum_tensor(f"ps_{k}{i}", [P, 512], F32))
                     for i in range(2 if k in "AB" else 1)] for k in "ABPQOX"}
        full = {k: sem(f"full_{k}") for k in banks}
        free = {k: sem(f"free_{k}") for k in banks}

        def psum(name, u, i=0):
            bank, n = where[name, u, i]
            return banks[bank][n % len(banks[bank])]

        def wait_free(eng, name, u, i=0):
            bank, n = where[name, u, i]
            if n + 1 > len(banks[bank]):
                eng.wait_ge(free[bank], n + 1 - len(banks[bank]))

        def wait_full(eng, name, u, i=0):
            bank, n = where[name, u, i]
            eng.wait_ge(full[bank], n + 1)

        def wait_done(eng, name, u, i=0):
            bank, n = where[name, u, i]
            eng.wait_ge(free[bank], n + 1)

        x_sb = sb("x_sb", [P, NB, P])
        xb_sb = sb("xb_sb", [P, NB, P])
        ctx_sb = sb("ctx_sb", [P, NB, P])
        m0_i = sb("m0_i", [P, NB, P], I32)
        m0T_i = sb("m0T_i", [P, NB, P], I32)
        m1_i = sb("m1_i", [P, P], I32)
        m1T_i = sb("m1T_i", [P, P], I32)
        m0_b = sb("m0_b", [P, NB, P], BF16)
        m0T_b = sb("m0T_b", [P, NB, P], BF16)
        m1_b = sb("m1_b", [P, P], BF16)
        m1T_b = sb("m1T_b", [P, P], BF16)
        wq_sb = [sb(f"wq{l}_sb", [P, P]) for l in range(2)]
        wkv_sb = [sb(f"wkv{l}_sb", [P, 2 * P]) for l in range(2)]
        wo_sb = [sb(f"wo{l}_sb", [P, P]) for l in range(2)]
        bo_sb = sb("bo_sb", [P, P])
        wf_sb = sb("wf_sb", [P, 3, INNER])
        wf_q = sb("wf_q", [P, 3, INNER], BF16)
        wf_t = sb("wf_t", [P, INNER])
        wf_sum = sb("wf_sum", [P, 3])
        wf_mean = sb("wf_mean", [P, 3])
        wf_inv = sb("wf_inv", [P, 3])
        wf_gu = sb("wf_gu", [P, 2])
        w1_sb = sb("w1_sb", [P, ZCH, P])
        w2_sb = sb("w2_sb", [P, ZCH, P])
        b1_sb = sb("b1_sb", [P, ZCH])
        b2_sb = sb("b2_sb", [P, E * P])
        b2_f = sb("b2_f", [P, E * P])
        b2_h = sb("b2_h", [P, E * P], BF16)
        b2_p = sb("b2_p", [P, E * P], BF16)
        gT_sb = sb("gT_sb", [P, E])
        gb_sb = sb("gb_sb", [P, E])
        cst_sb = sb("cst_sb", [P, C_N])
        id_b = sb("id_b", [P, P], BF16)
        rows3 = sb("rows3", [P, P], BF16)
        ones = sb("ones", [P, P])
        ident = cst_sb[:, C_ID:C_ID + P]
        w8 = cst_sb[:, C_W8:C_W8 + E]

        st6 = sb("st6", [P, 4, NB, 6])
        mv = sb("mv", [P, 4, NB, 2])
        hv = sb("hv", [P, 4, NB, 1])
        ry = sb("ry", [P, 4, NB, 4])
        rt = sb("rt", [P, 4, NB, 3])
        xh = sb("xh", [P, 4, 2, P])

        xT = sb("xT", [P, 2, P])
        qst = sb("qst", [P, 3, GROUPS, MROWS], BF16)
        kst = sb("kst", [P, 2, GROUPS, MROWS], BF16)
        qr = sb("qr", [P, 2, P])
        kr = sb("kr", [P, 2, P])
        v_sb = sb("v_sb", [P, 5, H, DH + 1])
        qT = sb("qT", [P, 2, GROUPS, P], BF16)
        qmT = sb("qmT", [P, 2, GROUPS, P], BF16)
        kT = sb("kT", [P, 2, GROUPS, P], BF16)
        kblk = sb("kblk", [P, 5, GROUPS, 2, P], BF16)
        mx = sb("mx", [P, 2, H])
        nm = sb("nm", [P, 2, 3, H])
        probs = sb("probs", [P, 2, H, P])
        oT_sb = sb("oT_sb", [P, 2, 4 * P])
        rden = sb("rden", [P, 2, H])
        attn = sb("attn", [P, 2, H, DH])
        aT_sb = sb("aT_sb", [P, 2, P])

        fs = sb("fs", [P, NB, 16])
        xr = sb("xr", [P, 2, P])
        xq = sb("xq", [P, 2, P], BF16)
        xqT = sb("xqT", [P, 2, P], BF16)
        th = sb("th", [P, INNER])
        gate_sb = sb("gate_sb", [P, INNER])
        z1 = sb("z1", [P, INNER])
        z2 = sb("z2", [P, 2, INNER])
        hr = sb("hr", [P, INNER])
        hq = sb("hq", [P, 2, INNER], BF16)
        hqT = sb("hqT", [P, 2, 4, P], BF16)

        mxT = sb("mxT", [P, 2, P])
        lg = sb("lg", [P, NB, 10, E])
        ls = sb("ls", [P, NB, 12])
        comb = sb("comb", [P, NB, E])
        hid = sb("hid", [P, 2, ZCH, P])
        yc = sb("yc", [P, 2, E, P])
        out_sb = sb("out_sb", [P, 2, P])

        s_cst, s_x, s_ctx, s_w0, s_mask, s_w1, s_wf, s_moe = [
            sem(n) for n in ("cst_in", "x_in", "ctx_in", "w0_in", "mask_in", "w1_in", "wf_in", "moe_in")]
        const_ready = sem("const_ready")
        mask_ready = sem("mask_ready")
        s_mask1 = sem("mask1_in")
        wsum_ready, wmean_ready, wq_ready = sem("wsum_ready"), sem("wmean_ready"), sem("wq_ready")
        b2_ready = sem("b2_ready")
        stats_ready = [sem(f"stats_ready{k}") for k in range(4)]
        rstd_ready = [sem(f"rstd_ready{k}") for k in range(4)]
        xh_ready = [sem(f"xh_ready{k}") for k in range(4)]
        xb_ready = sem("xb_ready")
        v_ready, qst_ready, kst_ready, kblk_ready, mpart_ready = [
            sem(n) for n in ("v_ready", "qst_ready", "kst_ready", "kblk_ready", "mpart_ready")]
        c_ready, xq_ready, z1_ready, hq_ready = [sem(n) for n in ("c_ready", "xq_ready", "z1_ready", "hq_ready")]
        d_ready, e_ready, out_ready = sem("d_ready"), sem("e_ready"), sem("out_ready")
        s_out = [sem("out_stored0"), sem("out_stored1")]
        dve_done, pool_done, act_done = sem("dve_done"), sem("pool_done"), sem("act_done")

        def ln(kind, u):
            return {"attn": 2 * (u // NB), "ffn": 1, "moe": 3}[kind], u % NB

        block = ctx.enter_context(nc.Block())

        @block.sync
        def _(sp):
            sp.dma_start(x_sb[:, 0, :], x[0]).then_inc(s_x, 16)
            sp.dma_start(cst_sb[:, :], cst).then_inc(s_cst, 16)
            sp.dma_start(ctx_sb[:, :, :], ctxT).then_inc(s_ctx, 16)
            sp.dma_start(wq_sb[0][:, :], w0q).then_inc(s_w0, 16)
            sp.dma_start(wkv_sb[0][:, :], w0kv).then_inc(s_w0, 16)
            sp.dma_start(x_sb[:, 1:NB, :], x[1:NB].rearrange("b t d -> t b d")).then_inc(s_x, 16)
            sp.dma_start(m0_i[:, :, :], mask0.rearrange("b q k -> q b k")).then_inc(s_mask, 16)
            sp.dma_start(m0T_i[:, :, :], mask0T).then_inc(s_mask, 16)
            sp.dma_start(m1_i[:, :], mask1).then_inc(s_mask1, 16)
            sp.dma_start(m1T_i[:, :], mask1T).then_inc(s_mask1, 16)
            sp.dma_start(wo_sb[0][:, :], w0o).then_inc(s_w0, 16)
            sp.dma_start(wf_sb[:, 0, :], wg).then_inc(s_wf, 16)
            sp.dma_start(wf_sb[:, 1, :], wu).then_inc(s_wf, 16)
            sp.dma_start(wf_sb[:, 2, :], wd).then_inc(s_wf, 16)
            for dst, src in ((wq_sb[1], w1q), (wkv_sb[1], w1kv), (wo_sb[1], w1o),
                             (bo_sb, bo.partition_broadcast(P))):
                sp.dma_start(dst[:, :], src).then_inc(s_w1, 16)
            sp.dma_start(w1_sb[:, :, :], m1T).then_inc(s_moe, 16)
            sp.dma_start(w2_sb[:, :, :], m2T).then_inc(s_moe, 16)
            sp.dma_start(b1_sb[:, :], mb1).then_inc(s_moe, 16)
            sp.dma_start(b2_sb[0:3, :], mb2.partition_broadcast(3)).then_inc(s_moe, 16)
            sp.dma_start(gT_sb[:, :], gT).then_inc(s_moe, 16)
            sp.dma_start(gb_sb[:, :], gb.partition_broadcast(P)).then_inc(s_moe, 16)
            for b in range(NB):
                sp.wait_ge(out_ready, b + 1)
                sp.dma_start(out[b], out_sb[:, b % 2, :]).then_inc(s_out[b % 2], 16)
            for half in s_out:
                sp.wait_ge(half, 8 * NB)

        @block.gpsimd
        def _(pool):
            done = [0]

            def chain(ins):
                done[0] += 1
                ins.then_inc(pool_done, 1)
                pool.wait_ge(pool_done, done[0])

            pool.memset(ones[:, :], 1.0).then_inc(const_ready, 1)
            pool.memset(kst[:, :, :, ROWS:MROWS], 1.0).then_inc(const_ready, 1)
            pool.memset(v_sb[:, :, :, DH:DH + 1], 1.0).then_inc(const_ready, 1)
            pool.memset(rows3[:, :], 0.0)
            pool.memset(b2_p[:, :], 0.0).then_inc(const_ready, 1)
            pool.wait_ge(const_ready, 4)
            pool.memset(rows3[0:3, :], 1.0).then_inc(const_ready, 1)

            def masks(b0, b1):
                if b0 == 0:
                    pool.wait_ge(s_mask, 32)
                for dst, src in ((m0_b, m0_i), (m0T_b, m0T_i)):
                    pool.tensor_scalar(dst[:, b0:b1, :], src[:, b0:b1, :], 0.0, MASKED, ALU.is_equal,
                                       ALU.mult).then_inc(mask_ready, 1)

            def masks_shared():
                pool.wait_ge(s_mask1, 32)
                for dst, src in ((m1_b, m1_i), (m1T_b, m1T_i)):
                    pool.tensor_scalar(dst[:, :], src[:, :], 0.0, MASKED, ALU.is_equal,
                                       ALU.mult).then_inc(mask_ready, 1)

            def rstd(kind, u):
                k, b = ln(kind, u)
                h, y, t = hv[:, k, b, 0:1], ry[:, k, b, :], rt[:, k, b, :]
                pool.wait_ge(stats_ready[k], b + 1)
                chain(pool.tensor_scalar(h, mv[:, k, b, 1:2], EPS, 0.5, ALU.add, ALU.mult))
                chain(pool.tensor_scalar(y[:, 0:1].bitcast(I32), h.bitcast(I32), -0.5, MAGIC, ALU.mult, ALU.add))
                for s in range(3):
                    chain(pool.tensor_scalar(t[:, s:s + 1], y[:, s:s + 1], y[:, s:s + 1], h, ALU.mult, ALU.mult))
                    last = pool.tensor_scalar(y[:, s + 1:s + 2], t[:, s:s + 1], 1.5, y[:, s:s + 1], ALU.subtract, ALU.mult)
                    if s < 2:
                        chain(last)
                last.then_inc(rstd_ready[k], 1)

            def sum_experts(b):
                y = yc[:, b % 2, :, :]
                wait_done(pool, "y", b, 1)
                for w in (4, 2, 1):
                    chain(pool.tensor_tensor(y[:, 0:w, :], y[:, 0:w, :], y[:, w:2 * w, :], ALU.add))
                if b >= 2:
                    pool.wait_ge(s_out[b % 2], 16 * (b // 2))
                pool.tensor_tensor(out_sb[:, b % 2, :], y[:, 0, :], x_sb[:, b, :], ALU.add).then_inc(out_ready, 1)

            for name, n, _ in timeline(POOL_AT):
                b = n % NB
                if n == 0 and name == "masks": masks(0, 1)
                if n == 1 and name == "masks": masks(1, NB)
                if n == NB and name == "masks": masks_shared()
                if name == "sum": sum_experts(b)
                if name == "rstd":
                    rstd("attn", n)
                if name == "frstd":
                    rstd("ffn" if n < NB else "moe", b)
                if name == "rstd" and n >= NB:
                    if b == 0:
                        pool.wait_ge(s_w1, 64)
                    pool.tensor_tensor(xb_sb[:, b, :], x_sb[:, b, :], bo_sb[:, :], ALU.add).then_inc(xb_ready, 1)

        @block.tensor
        def _(pe):
            def filled(mm, name, u, i=0):
                mm.then_inc(full[where[name, u, i][0]], 1)

            def maxima_scores(n, i):
                l, b = n // NB, n % NB
                o = psum("max", n, i)
                if i == 0:
                    wait_done(pe, "qs", n)
                    pe.wait_ge(kblk_ready, n + 1)
                if i == 0 and n in (0, 1, NB):
                    pe.wait_ge(mask_ready, {0: 2, 1: 4, NB: 6}[n])
                wait_free(pe, "max", n, i)
                m = (m0_b[:, b, :] if l == 0 else m1_b[:, :]).unsqueeze(1).broadcast_to([P, 4, P])
                pe.matmul(o[:, :].rearrange("p (h k) -> p h k", h=4), id_b[:, :], m, start=True, stop=False)
                for g in (2 * i, 2 * i + 1):
                    mm = pe.matmul(o[:, 256 * (g % 2):256 * (g % 2) + 256], qT[0:ROWS, n % 2, g, :],
                                   kblk[0:ROWS, n % 5, g, :, :].rearrange("p a b -> p (a b)"),
                                   start=False, stop=(g % 2 == 1))
                filled(mm, "max", n, i)

            def shifted_scores(n, i):
                l, b = n // NB, n % NB
                o = psum("exp", n, i)
                if i == 0:
                    wait_done(pe, "qb", n)
                wait_free(pe, "exp", n, i)
                m = (m0T_b[:, b, :] if l == 0 else m1T_b[:, :]).unsqueeze(1).broadcast_to([P, 4, P])
                pe.matmul(o[:, :].rearrange("p (h k) -> p h k", h=4), id_b[:, :], m, start=True, stop=False)
                for h in range(4 * i, 4 * i + 4):
                    mm = pe.matmul(o[:, P * (h % 4):P * (h % 4 + 1)], kblk[0:MROWS, n % 5, h // 2, h % 2, :],
                                   qmT[0:MROWS, n % 2, h // 2, :], start=False, stop=(h % 4 == 3))
                filled(mm, "exp", n, i)

            def turn(name, u, src, idn, dt=F32):
                wait_free(pe, name, u)
                o = psum(name, u)
                o = o[:, 0:P] if dt == F32 else o[:, 0:P // 2].bitcast(BF16)
                filled(pe.transpose(o, src, idn), name, u)

            def qkv(n):
                l, b = n // NB, n % NB
                if n == 0:
                    pe.wait_ge(s_w0, 48)
                    pe.wait_ge(s_ctx, 16)
                if n == NB:
                    pe.wait_ge(s_w1, 64)
                wait_free(pe, "qkv", n)
                o = psum("qkv", n)
                pe.matmul(o[:, P:3 * P], ctx_sb[:, b, :], wkv_sb[l][:, :], start=True, stop=True)
                wait_done(pe, "xT", n)
                filled(pe.matmul(o[:, 0:P], xT[:, n % 2, :], wq_sb[l][:, :], start=True, stop=True), "qkv", n)

            def stack(name, n, src, rows):
                wait_free(pe, name, n)
                o = psum(name, n)[:, :].bitcast(BF16)
                for g in range(GROUPS):
                    mm = pe.transpose(o[0:rows, g * P:(g + 1) * P], src[:, g, 0:rows], id_b[:, :])
                filled(mm, name, n)

            def weighted_values(n):
                wait_free(pe, "pv", n)
                pe.wait_ge(v_ready, n + 1)
                wait_done(pe, "exp", n, 3)
                o = psum("pv", n)
                for h in range(H):
                    j = h % 4
                    mm = pe.matmul(o[32 * j:32 * j + DH + 1, (h // 4) * P:(h // 4 + 1) * P], v_sb[:, n % 5, h, :],
                                   probs[:, n % 2, h, :], start=True, stop=True)
                filled(mm, "pv", n)

            def turn_outputs(n):
                wait_free(pe, "oT", n)
                wait_done(pe, "pv", n)
                o = psum("oT", n)
                for g in range(4):
                    mm = pe.transpose(o[:, g * P:(g + 1) * P], oT_sb[:, n % 2, g * P:(g + 1) * P], ident)
                filled(mm, "oT", n)

            def project(n):
                wait_free(pe, "wo", n)
                wait_done(pe, "aT", n)
                filled(pe.matmul(psum("wo", n)[:, 0:P], aT_sb[:, n % 2, :], wo_sb[n // NB][:, :],
                                 start=True, stop=True), "wo", n)

            def gate_up(name, b):
                if b == 0:
                    pe.wait_ge(wq_ready, 3)
                wait_done(pe, "fxT", b)
                wait_free(pe, name, b)
                k = ("gate", "up").index(name)
                filled(pe.matmul(psum(name, b)[:, :], xqT[:, b % 2, :], wf_q[:, k, :], start=True, stop=True), name, b)

            def turn_hidden(b):
                wait_free(pe, "hT", b)
                pe.wait_ge(hq_ready, b + 1)
                o = psum("hT", b)[:, 0:256].bitcast(BF16)
                for c in range(4):
                    mm = pe.transpose(o[:, c * P:(c + 1) * P], hq[:, b % 2, c * P:(c + 1) * P], id_b[:, :])
                filled(mm, "hT", b)

            def down(b):
                wait_free(pe, "down", b)
                wait_done(pe, "hT", b)
                for c in range(4):
                    mm = pe.matmul(psum("down", b)[:, 0:P], hqT[:, b % 2, c, :], wf_q[:, 2, c * P:(c + 1) * P],
                                   start=(c == 0), stop=(c == 3))
                filled(mm, "down", b)

            def logits(b):
                if b == 0:
                    pe.wait_ge(s_moe, 96)
                wait_free(pe, "logit", b)
                wait_done(pe, "mxT", b)
                filled(pe.matmul(psum("logit", b)[:, 0:E], mxT[:, b % 2, :], gT_sb[:, :], start=True, stop=True), "logit", b)

            def hidden(b, i):
                if i == 0:
                    wait_done(pe, "mxT", b)
                wait_free(pe, "z", b, i)
                for c in range(4):
                    mm = pe.matmul(psum("z", b, i)[:, c * P:(c + 1) * P], w1_sb[:, 4 * i + c, :], mxT[:, b % 2, :],
                                   start=True, stop=True)
                filled(mm, "z", b, i)

            def experts(b, i):
                if b == 0 and i == 0:
                    pe.wait_ge(b2_ready, 1)
                    pe.wait_ge(const_ready, 5)
                wait_free(pe, "y", b, i)
                o = psum("y", b, i)
                pe.matmul(o[:, :], rows3[:, :], b2_p[:, i * 512:(i + 1) * 512], start=True, stop=False)
                wait_done(pe, "z", b, 2 * i + 1)
                for c in range(8 * i, 8 * i + 8):
                    e = c // 2 - 4 * i
                    mm = pe.matmul(o[:, e * P:(e + 1) * P], hid[:, b % 2, c, :], w2_sb[:, c, :],
                                   start=False, stop=(c == 8 * i + 7))
                filled(mm, "y", b, i)

            pe.wait_ge(s_cst, 16)
            pe.wait_ge(dve_done, 1)
            for name, n, i in timeline(PE_AT):
                u = n % NB if name in PER_BATCH else n
                if name == "max": maxima_scores(u, i)
                if name == "exp": shifted_scores(u, i)
                if name == "xT":
                    k, b = ln("attn", u)
                    pe.wait_ge(xh_ready[k], b + 1)
                    turn("xT", u, xh[:, k, b % 2, :], ident)
                if name == "fxT":
                    pe.wait_ge(xq_ready, u + 1)
                    turn("fxT", u, xq[:, u % 2, :], id_b[:, :], BF16)
                if name == "mxT":
                    pe.wait_ge(xh_ready[3], u + 1)
                    turn("mxT", u, xh[:, 3, u % 2, :], ident)
                if name == "qkv": qkv(u)
                if name == "ks":
                    pe.wait_ge(kst_ready, u + 1)
                    stack("ks", u, kst[:, u % 2, :, :], MROWS)
                if name == "qs":
                    pe.wait_ge(qst_ready, u + 1)
                    stack("qs", u, qst[:, u % 3, :, :], ROWS)
                if name == "qb":
                    pe.wait_ge(mpart_ready, u + 1)
                    stack("qb", u, qst[:, u % 3, :, :], MROWS)
                if name == "pv": weighted_values(u)
                if name == "oT": turn_outputs(u)
                if name == "aT":
                    wait_done(pe, "oT", u)
                    turn("aT", u, attn[:, u % 2, :, :].rearrange("p h d -> p (h d)"), ident)
                if name == "wo": project(u)
                if name in ("gate", "up"): gate_up(name, u)
                if name == "hT": turn_hidden(u)
                if name == "down": down(u)
                if name == "logit": logits(u)
                if name == "z": hidden(u, i)
                if name == "y": experts(u, i)
                if name == "max" and u == 0 and i == 0:
                    pe.wait_ge(wsum_ready, 3)
                    pe.wait_ge(const_ready, 5)
                    pe.wait_ge(dve_done, 2)
                    pe.matmul(banks["X"][0][:, 0:3], ones[:, :], wf_sum[:, :], start=True, stop=True).then_inc(wmean_ready, 1)

        @block.scalar
        def _(act):
            def freed(ins, name, u, i=0):
                ins.then_inc(free[where[name, u, i][0]], 1)

            def evacuate(dst, name, u, src):
                wait_full(act, name, u)
                ins = act.activation(dst, src, ACT.Copy)
                freed(ins, name, u)

            def high_parts(n):
                wait_full(act, "qkv", n)
                o = psum("qkv", n)
                if n >= 3:
                    act.wait_ge(full["Q"], where["qb", n - 3, 0][1] + 1)
                if n >= 2:
                    act.wait_ge(full["Q"], where["ks", n - 2, 0][1] + 1)
                if n == 0:
                    act.wait_ge(const_ready, 5)
                grp = lambda ap: ap.rearrange("p (g r) -> p g r", g=GROUPS)
                for c in range(3):
                    act.activation(qst[:, n % 3, :, (3 + c) * PAIR:(4 + c) * PAIR], grp(o[:, 0:P]), ACT.Copy)
                for c in range(3):
                    act.activation(kst[:, n % 2, :, (1 + c) * PAIR:(2 + c) * PAIR], grp(o[:, P:2 * P]), ACT.Copy)
                if n >= 5:
                    act.wait_ge(full["O"], where["pv", n - 5, 0][1] + 1)
                act.activation(v_sb[:, n % 5, :, 0:DH], o[:, 2 * P:3 * P].rearrange("p (h d) -> p h d", h=H),
                               ACT.Copy).then_inc(v_ready, 1)

            def exps(n, i):
                wait_full(act, "exp", n, i)
                if n >= 2 and i == 0:
                    act.wait_ge(full["O"], where["pv", n - 2, 0][1] + 1)
                ins = act.activation(probs[:, n % 2, 4 * i:4 * i + 4, :],
                                     psum("exp", n, i)[:, :].rearrange("p (h k) -> p h k", h=4),
                                     ACT.Exp, scale=ATTN_SCALE[n // NB])
                freed(ins, "exp", n, i)

            def relu(b, i):
                wait_full(act, "z", b, i)
                if b >= 2 and i == 0:
                    act.wait_ge(full["A"], where["y", b - 2, 1][1] + 1)
                for c in range(4):
                    ins = act.activation(hid[:, b % 2, 4 * i + c, :], psum("z", b, i)[:, c * P:(c + 1) * P],
                                         ACT.Relu, bias=b1_sb[:, 4 * i + c:4 * i + c + 1])
                freed(ins, "z", b, i)

            for name, n, i in timeline(PE_AT, ACT_LAG, ACT_AT):
                u = n % NB if name in PER_BATCH or name == "e" else n
                if name == "exp": exps(u, i)
                if name == "xT":
                    if u >= 2:
                        act.wait_ge(full["P"], where["qkv", u - 2, 0][1] + 1)
                    evacuate(xT[:, u % 2, :], "xT", u, psum("xT", u)[:, 0:P])
                if name == "fxT":
                    if u >= 2:
                        act.wait_ge(full["A"], where["up", u - 2, 0][1] + 1)
                    evacuate(xqT[:, u % 2, :], "fxT", u, psum("fxT", u)[:, 0:P // 2].bitcast(BF16))
                if name == "mxT":
                    if u >= 2:
                        act.wait_ge(full["B"], where["z", u - 2, 3][1] + 1)
                    evacuate(mxT[:, u % 2, :], "mxT", u, psum("mxT", u)[:, 0:P])
                if name == "qkv": high_parts(u)
                if name == "qs":
                    if u >= 2:
                        act.wait_ge(full["A"], where["max", u - 2, 3][1] + 1)
                    evacuate(qT[0:ROWS, u % 2, :, :].rearrange("p g k -> p (g k)"), "qs", u,
                             psum("qs", u)[0:ROWS, :].bitcast(BF16))
                if name == "ks":
                    if u >= 2:
                        act.wait_ge(kblk_ready, u - 1)
                    evacuate(kT[0:MROWS, u % 2, :, :].rearrange("p g k -> p (g k)"), "ks", u,
                             psum("ks", u)[0:MROWS, :].bitcast(BF16))
                if name == "pv":
                    if u >= 2:
                        act.wait_ge(full["O"], where["oT", u - 2, 0][1] + 1)
                    if u == 0:
                        act.wait_ge(const_ready, 5)
                    evacuate(oT_sb[:, u % 2, :], "pv", u, psum("pv", u)[:, :])
                if name == "aT":
                    if u >= 2:
                        act.wait_ge(full["O"], where["wo", u - 2, 0][1] + 1)
                    evacuate(aT_sb[:, u % 2, :], "aT", u, psum("aT", u)[:, 0:P])
                if name == "gate":
                    wait_full(act, "gate", u)
                    act.wait_ge(c_ready, u + 1)
                    if u >= 1:
                        wait_done(act, "up", u - 1)
                    act.activation(th[:, :], psum("gate", u)[:, :], ACT.Tanh, scale=fs[:, u, 4:5])
                    freed(act.activation(gate_sb[:, :], psum("gate", u)[:, :], ACT.Copy), "gate", u)
                if name == "hT":
                    if u >= 2:
                        act.wait_ge(full["X"], where["down", u - 2, 0][1] + 1)
                    evacuate(hqT[:, u % 2, :, :].rearrange("p c t -> p (c t)"), "hT", u,
                             psum("hT", u)[:, 0:256].bitcast(BF16))
                if name == "z": relu(u, i)
                if name == "e":
                    act.wait_ge(d_ready, u + 1)
                    act.activation(ls[:, u, 5:6], ls[:, u, 4:5], ACT.Exp).then_inc(e_ready, 1)

        @block.vector
        def _(dve):
            done = [0]

            def mark(ins):
                done[0] += 1
                ins.then_inc(dve_done, 1)
                return done[0]

            def chain(ins):
                dve.wait_ge(dve_done, mark(ins))

            def freed(ins, name, u, i=0):
                ins.then_inc(free[where[name, u, i][0]], 1)

            def stats(kind, u):
                k, b = ln(kind, u)
                if u == 0 or (k == 0 and b == 1):
                    dve.wait_ge(s_x, 16 if b == 0 else 32)
                chain(dve.bn_stats(st6[:, k, b, :], x_sb[:, b, :]))
                dve.bn_aggr(mv[:, k, b, :], st6[:, k, b, :]).then_inc(stats_ready[k], 1)

            def normalise(kind, u):
                k, b = ln(kind, u)
                dve.wait_ge(rstd_ready[k], b + 1)
                if b >= 2:
                    if k in (0, 2):
                        dve.wait_ge(full["P"], where["xT", u - 2, 0][1] + 1)
                    if k == 3:
                        dve.wait_ge(full["P"], where["mxT", u - 2, 0][1] + 1)
                ins = dve.tensor_scalar(xh[:, k, b % 2, :], x_sb[:, b, :], mv[:, k, b, 0:1], ry[:, k, b, 3:4],
                                        ALU.subtract, ALU.mult)
                ins.then_inc(xh_ready[k], 1)

            def low_parts(n):
                o = psum("qkv", n)
                grp = lambda ap: ap.rearrange("p (g r) -> p g r", g=GROUPS)
                dve.wait_ge(v_ready, n + 1)
                st, i = qst[:, n % 3, :, :], n % 2
                dve.tensor_tensor(grp(qr[:, i, :]), grp(o[:, 0:P]), st[:, :, 3 * PAIR:4 * PAIR], ALU.subtract)
                kk = kst[:, i, :, :]
                ins = dve.tensor_tensor(grp(kr[:, i, :]), grp(o[:, P:2 * P]), kk[:, :, PAIR:2 * PAIR], ALU.subtract)
                freed(ins, "qkv", n)
                wait_done(dve, "qkv", n)
                two = lambda ap: ap.rearrange("p (g a r) -> p g a r", g=GROUPS, a=1).broadcast_to([P, GROUPS, 2, PAIR])
                dve.tensor_copy(st[:, :, 0:2 * PAIR].rearrange("p g (c r) -> p g c r", c=2), two(qr[:, i, :]))
                dve.tensor_copy(kk[:, :, 0:PAIR], grp(kr[:, i, :]))
                chain(dve.tensor_copy(kk[:, :, 4 * PAIR:5 * PAIR], grp(kr[:, i, :])))
                dve.tensor_tensor(st[:, :, 2 * PAIR:3 * PAIR], grp(qr[:, i, :]), st[:, :, 0:PAIR],
                                  ALU.subtract).then_inc(qst_ready, 1)
                dve.tensor_tensor(kk[:, :, 5 * PAIR:6 * PAIR], grp(kr[:, i, :]), kk[:, :, 0:PAIR],
                                  ALU.subtract).then_inc(kst_ready, 1)

            def key_blocks(n):
                wait_done(dve, "ks", n)
                if n >= 5:
                    dve.wait_ge(full["B"], where["exp", n - 5, 3][1] + 1)
                for j in range(2):
                    ins = dve.tensor_scalar(kblk[0:MROWS, n % 5, :, j, :], kT[0:MROWS, n % 2, :, :],
                                            cst_sb[0:MROWS, C_SEL + j:C_SEL + j + 1], None, ALU.mult)
                ins.then_inc(kblk_ready, 1)

            def shifted_queries(n):
                wait_full(dve, "qb", n)
                if n >= 2:
                    dve.wait_ge(full["B"], where["exp", n - 2, 3][1] + 1)
                freed(dve.tensor_copy(qmT[0:MROWS, n % 2, :, :].rearrange("p g k -> p (g k)"),
                                      psum("qb", n)[0:MROWS, :].bitcast(BF16)), "qb", n)

            def maxima(n, i):
                wait_full(dve, "max", n, i)
                ins = dve.tensor_reduce(mx[:, n % 2, 4 * i:4 * i + 4],
                                        psum("max", n, i)[:, :].rearrange("p (h k) -> p h k", h=4), AX.X, ALU.max)
                freed(ins, "max", n, i)

            def maxima_parts(n):
                wait_done(dve, "max", n, 3)
                i = n % 2
                st = qst[:, n % 3, :, ROWS:MROWS].rearrange("p g (j c) -> p g j c", j=2)
                hd = lambda ap: ap.rearrange("p (g j) -> p g j", j=2)
                m = [hd(nm[:, i, c, :]) for c in range(3)]
                chain(dve.tensor_scalar(nm[:, i, 0, :], mx[:, i, :], -1.0, None, ALU.mult))
                chain(dve.tensor_copy(st[:, :, :, 0], m[0]))
                chain(dve.tensor_tensor(m[1], m[0], st[:, :, :, 0], ALU.subtract))
                chain(dve.tensor_copy(st[:, :, :, 1], m[1]))
                dve.tensor_tensor(st[:, :, :, 2], m[1], st[:, :, :, 1], ALU.subtract).then_inc(mpart_ready, 1)

            def divide(n):
                wait_full(dve, "oT", n)
                o = psum("oT", n)[:, :].rearrange("p (h r) -> p h r", h=H)
                i = n % 2
                chain(dve.reciprocal(rden[:, i, :].unsqueeze(2), o[:, :, DH:DH + 1]))
                if n >= 2:
                    dve.wait_ge(full["O"], where["aT", n - 2, 0][1] + 1)
                ins = dve.tensor_tensor(attn[:, i, :, :], o[:, :, 0:DH],
                                        rden[:, i, :].unsqueeze(2).broadcast_to([P, H, DH]), ALU.mult)
                freed(ins, "oT", n)

            def add_attention(n):
                b = n % NB
                wait_full(dve, "wo", n)
                if n >= NB:
                    dve.wait_ge(xb_ready, b + 1)
                res = x_sb[:, b, :] if n < NB else xb_sb[:, b, :]
                ins = dve.tensor_tensor(x_sb[:, b, :], psum("wo", n)[:, 0:P], res, ALU.add)
                freed(ins, "wo", n)
                wait_done(dve, "wo", n)

            def quantise_x(b):
                i = b % 2
                f = lambda c: fs[:, b, c:c + 1]
                dve.wait_ge(xh_ready[1], b + 1)
                chain(dve.tensor_reduce(f(0), xh[:, 1, i, :], AX.X, ALU.max, apply_absolute_value=True))
                chain(dve.tensor_scalar(f(1), f(0), EPS, None, ALU.max))
                if b == 0:
                    dve.wait_ge(wq_ready, 3)
                dve.tensor_scalar(f(4), f(1), wf_gu[:, 0:1], None, ALU.mult).then_inc(c_ready, 1)
                dve.tensor_scalar(f(5), f(1), f(1), wf_gu[:, 1:2], ALU.mult, ALU.mult)
                chain(dve.reciprocal(f(2), f(1)))
                chain(dve.tensor_scalar(f(3), f(2), QMAX, None, ALU.mult))
                chain(dve.tensor_scalar(xr[:, i, :], xh[:, 1, i, :], f(3), ROUND, ALU.mult, ALU.add))
                if b >= 2:
                    dve.wait_ge(full["P"], where["fxT", b - 2, 0][1] + 1)
                dve.tensor_scalar(xq[:, i, :], xr[:, i, :], ROUND, QMAX, ALU.subtract, ALU.min).then_inc(xq_ready, 1)

            def silu_gate(b):
                wait_done(dve, "gate", b)
                dve.scalar_tensor_tensor(out=z1[:, :], in0=th[:, :], scalar=1.0, in1=gate_sb[:, :],
                                         op0=ALU.add, op1=ALU.mult).then_inc(z1_ready, 1)

            def times_up(b):
                wait_full(dve, "up", b)
                dve.wait_ge(z1_ready, b + 1)
                ins = dve.tensor_tensor(z2[:, b % 2, :], z1[:, :], psum("up", b)[:, :], ALU.mult)
                freed(ins, "up", b)

            def quantise_h(b):
                i = b % 2
                f = lambda c: fs[:, b, c:c + 1]
                wait_done(dve, "up", b)
                chain(dve.tensor_reduce(f(7), z2[:, i, :], AX.X, ALU.max, apply_absolute_value=True))
                chain(dve.tensor_scalar(f(8), f(7), f(5), EPS, ALU.mult, ALU.max))
                dve.tensor_scalar(f(13), f(8), wf_mean[:, 2:3], 1.0 / QMAX, ALU.mult, ALU.mult)
                chain(dve.reciprocal(f(10), f(8)))
                chain(dve.tensor_scalar(f(11), f(10), QMAX, f(5), ALU.mult, ALU.mult))
                chain(dve.tensor_scalar(hr[:, :], z2[:, i, :], f(11), ROUND, ALU.mult, ALU.add))
                if b >= 2:
                    dve.wait_ge(full["X"], where["hT", b - 2, 0][1] + 1)
                dve.tensor_scalar(hq[:, i, :], hr[:, :], ROUND, QMAX, ALU.subtract, ALU.min).then_inc(hq_ready, 1)

            def add_ffn(b):
                wait_full(dve, "down", b)
                ins = dve.scalar_tensor_tensor(out=x_sb[:, b, :], in0=psum("down", b)[:, 0:P], scalar=fs[:, b, 13:14],
                                               in1=x_sb[:, b, :], op0=ALU.mult, op1=ALU.add)
                freed(ins, "down", b)
                wait_done(dve, "down", b)

            def top2(b):
                L = lambda c: lg[:, b, c, :]
                s = lambda c: ls[:, b, c:c + 1]
                wait_full(dve, "logit", b)
                if b == 0:
                    dve.wait_ge(s_moe, 96)
                ins = dve.tensor_tensor(L(0), psum("logit", b)[:, 0:E], gb_sb[:, :], ALU.add)
                freed(ins, "logit", b)
                wait_done(dve, "logit", b)
                for r in range(2):
                    v, key, hot = s(2 * r), s(2 * r + 1), L(3 * r + 2)
                    chain(dve.tensor_reduce(v, L(3 * r), AX.X, ALU.max))
                    chain(dve.scalar_tensor_tensor(out=L(3 * r + 1), in0=L(3 * r), scalar=v, in1=w8,
                                                   op0=ALU.is_ge, op1=ALU.mult))
                    chain(dve.tensor_reduce(key, L(3 * r + 1), AX.X, ALU.max))
                    chain(dve.tensor_scalar(hot, w8, key, None, ALU.is_equal))
                    if r == 0:
                        chain(dve.scalar_tensor_tensor(out=L(3), in0=hot, scalar=-3.0e38, in1=L(0),
                                                       op0=ALU.mult, op1=ALU.add))
                dve.tensor_scalar(s(4), s(2), s(0), None, ALU.subtract).then_inc(d_ready, 1)

            def combine(b):
                L = lambda c: lg[:, b, c, :]
                s = lambda c: ls[:, b, c:c + 1]
                dve.wait_ge(e_ready, b + 1)
                chain(dve.tensor_scalar(s(6), s(5), 1.0, None, ALU.add))
                chain(dve.reciprocal(s(7), s(6)))
                chain(dve.tensor_scalar(s(8), s(5), s(7), None, ALU.mult))
                chain(dve.tensor_scalar(L(8), L(2), s(7), None, ALU.mult))
                chain(dve.scalar_tensor_tensor(out=comb[:, b, :], in0=L(5), scalar=s(8), in1=L(8),
                                               op0=ALU.mult, op1=ALU.add))

            def weigh(b, i):
                wait_full(dve, "y", b, i)
                if b >= 2 and i == 0:
                    dve.wait_ge(out_ready, b - 1)
                freed(dve.tensor_tensor(yc[:, b % 2, 4 * i:4 * i + 4, :],
                                        psum("y", b, i)[:, :].rearrange("p (e o) -> p e o", e=4),
                                        comb[:, b, 4 * i:4 * i + 4].unsqueeze(2).broadcast_to([P, 4, P]),
                                        ALU.mult), "y", b, i)

            def sum_weights():
                dve.wait_ge(s_wf, 48)
                for k in range(3):
                    dve.tensor_reduce(wf_sum[:, k:k + 1], wf_sb[:, k, :], AX.X, ALU.add,
                                      apply_absolute_value=True).then_inc(wsum_ready, 1)

            def ternary_weights():
                dve.wait_ge(wmean_ready, 1)
                chain(dve.tensor_scalar(wf_mean[:, :], banks["X"][0][:, 0:3], 1.0 / (P * INNER), EPS, ALU.mult, ALU.max))
                chain(dve.reciprocal(wf_inv[:, :], wf_mean[:, :]))
                dve.tensor_scalar(wf_gu[:, 0:1], wf_mean[:, 0:1], 0.5 / QMAX, None, ALU.mult)
                chain(dve.tensor_scalar(wf_gu[:, 1:2], wf_mean[:, 0:1], wf_mean[:, 1:2], 0.5 / QMAX / QMAX, ALU.mult, ALU.mult))
                for k in range(3):
                    if k:
                        dve.wait_ge(wq_ready, k)
                    chain(dve.tensor_scalar(wf_t[:, :], wf_sb[:, k, :], wf_inv[:, k:k + 1], ROUND, ALU.mult, ALU.add))
                    chain(dve.tensor_scalar(wf_t[:, :], wf_t[:, :], ROUND, 1.0, ALU.subtract, ALU.min))
                    dve.tensor_scalar(wf_q[:, k, :], wf_t[:, :], -1.0, None, ALU.max).then_inc(wq_ready, 1)

            def bias_parts():
                dve.wait_ge(s_moe, 96)
                dve.wait_ge(const_ready, 5)
                r3 = lambda ap: ap[0:3, :]
                for sel, src in ((C_R12, b2_sb), (C_R2, b2_f)):
                    chain(dve.tensor_copy(r3(b2_h), r3(src)))
                    chain(dve.scalar_tensor_tensor(out=r3(b2_f), in0=r3(b2_h), scalar=r3(cst_sb)[:, sel:sel + 1],
                                                   in1=r3(src), op0=ALU.mult, op1=ALU.add))
                dve.tensor_copy(r3(b2_p), r3(b2_f)).then_inc(b2_ready, 1)

            dve.wait_ge(s_cst, 16)
            mark(dve.tensor_copy(id_b[:, :], ident))
            mark(dve.memset(banks["O"][0][:, :], 0.0))
            stats("attn", 0)
            normalise("attn", 0)
            for name, n, i in timeline(PE_AT, DVE_LAG, DVE_AT):
                b = n % NB
                if name == "stats" and n: stats("attn", n)
                if name == "norm" and n: normalise("attn", n)
                if name == "qkv":
                    low_parts(n)
                    if n == 0:
                        sum_weights()
                    if n == 1:
                        ternary_weights()
                    if n == NB:
                        bias_parts()
                if name == "kblk": key_blocks(n)
                if name == "max": maxima(n, i)
                if name == "parts": maxima_parts(n)
                if name == "qb": shifted_queries(n)
                if name == "oT": divide(n)
                if name == "wo":
                    add_attention(n)
                    stats("ffn" if n < NB else "moe", b)
                if name == "fnorm": normalise("ffn" if n < NB else "moe", b)
                if name == "qx": quantise_x(b)
                if name == "z1": silu_gate(b)
                if name == "up": times_up(b)
                if name == "qh": quantise_h(b)
                if name == "down":
                    add_ffn(b)
                    stats("attn", NB + b)
                if name == "top": top2(b)
                if name == "comb": combine(b)
                if name == "y": weigh(b, i)


_ORDER = ["x", "ctxT", "mask0", "mask0T", "mask1", "mask1T", "w0q", "w0kv", "w0o", "w1q", "w1kv", "w1o", "bo",
          "wg", "wu", "wd", "m1T", "mb1", "m2T", "mb2", "gT", "gb", "cst"]


def kernel(**inputs):
    import numpy as np
    import concourse.bacc as bacc
    from concourse.bass_utils import run_bass_kernel_spmd

    a = {k: np.asarray(v) for k, v in inputs.items()}

    def per_head(w):
        big = np.zeros((P, P), w.dtype)
        for h in range(H):
            big[h * DH:(h + 1) * DH, h * DH:(h + 1) * DH] = w.T
        return big

    cst = np.zeros((P, C_N), np.float32)
    cst[:, C_ID:C_ID + P] = np.eye(P)
    for r in range(MROWS):
        cst[r, C_SEL + ((r % PAIR) // DH if r < ROWS else (r - ROWS) // 3)] = 1.0
    cst[:, C_W8:C_W8 + E] = np.arange(E, 0, -1)
    cst[1:3, C_R12] = -1.0
    cst[2:3, C_R2] = -1.0
    data = {
        "x": a["x"],
        "ctxT": a["ctx_1024"].transpose(2, 0, 1),
        "mask0": a["mask_BxSxS2_ik1"],
        "mask0T": a["mask_BxSxS2_ik1"].transpose(2, 0, 1),
        "mask1": a["mask_1x1xSxS2_ik1"][0, 0],
        "mask1T": a["mask_1x1xSxS2_ik1"][0, 0].T,
        "w0q": a["L0_xattn_Wq"].T,
        "w0kv": np.concatenate([a["L0_xattn_Wk"].T, a["L0_xattn_Wv"].T], axis=1),
        "w0o": a["L0_xattn_Wo"].T,
        "w1q": per_head(a["L1_xattn_Wq"]),
        "w1kv": np.concatenate([per_head(a["L1_xattn_Wk"]), per_head(a["L1_xattn_Wv"])], axis=1),
        "w1o": a["L1_xattn_Wo"].T,
        "bo": a["L1_xattn_bo"],
        "wg": a["L0_ffn_w_gate"].T,
        "wu": a["L0_ffn_w_up"].T,
        "wd": a["L0_ffn_w_down"].T.reshape(INNER // P, P, P).transpose(1, 0, 2).reshape(P, INNER),
        "m1T": a["L1_ffn_W1"].reshape(ZCH, P, P).transpose(2, 0, 1),
        "mb1": a["L1_ffn_b1"].reshape(ZCH, P).T,
        "m2T": a["L1_ffn_W2"].transpose(0, 2, 1).reshape(ZCH, P, P).transpose(1, 0, 2),
        "mb2": a["L1_ffn_b2"].reshape(E * P),
        "gT": a["L1_ffn_Wg"].T,
        "gb": a["L1_ffn_bg"],
        "cst": cst,
    }
    nc = bacc.Bacc("TRN2", target_bir_lowering=False, num_devices=1)
    arrays, args = {}, []
    for name in _ORDER:
        v = np.ascontiguousarray(data[name])
        arrays[f"in_{name}"] = v
        args.append(nc.dram_tensor(f"in_{name}", v.shape, mybir.dt.from_np(v.dtype), kind="ExternalInput").ap())
    args.append(nc.dram_tensor("out_y", (NB, P, P), F32, kind="ExternalOutput").ap())
    build(nc, *args)
    r = run_bass_kernel_spmd(nc, [arrays], core_ids=[0])
    return r.results[0]["out_y"]
```

```python
from contextlib import ExitStack

import concourse.bass as bass
from concourse import mybir

F32 = mybir.dt.float32
BF16 = mybir.dt.bfloat16
I32 = mybir.dt.int32
ALU = mybir.AluOpType
ACT = mybir.ActivationFunctionType
AX = mybir.AxisListType

P = 128
NB = 8
H, DH = 16, 8
UNITS = 2 * NB
GROUPS = H // 2
PAIR = 2 * DH
PARTS = 6
ROWS = PARTS * PAIR
MROWS = ROWS + 6
INNER = 512
E, HID = 8, 256
ZCH = E * HID // P
MASKED = -(2.0 ** 100)
KSLOTS = 5
EPS = 1e-5
ROUND = 12582912.0
MAGIC = -554214945.0
QMAX = 127.0
ATTN_SCALE = (DH ** -0.5, P ** -0.5)

BANK = {"max": "A", "gate": "B", "up": "A", "y": "A", "exp": "B", "z": "B", "xT": "P", "qkv": "P", "fxT": "P",
        "mxT": "P", "qb": "Q", "ks": "Q", "qs": "Q", "pv": "O", "oT": "O", "aT": "O", "wo": "O",
        "hT": "X", "down": "X", "logit": "X"}
PER_BATCH = ("fxT", "gate", "up", "hT", "down", "mxT", "logit", "z", "y")

C_ID, C_SEL, C_IOTA, C_FROM1, C_FROM2 = 0, P, P + 2, P + 2 + E, P + 3 + E
C_N = P + 4 + E


UNIT_ORDER = ((0, 0), (0, 1), (0, 2), (0, 3), (0, 4), (0, 5), (1, 0), (0, 6),
              (1, 1), (0, 7), (1, 2), (1, 3), (1, 4), (1, 5), (1, 6), (1, 7))

ATTENTION = (
    ("pe.xT", 1, "pool.norm"),
    ("act.xT", 1, "pe.xT"),
    ("pe.qkv", 1, "act.xT"),
    ("act.qkv", 1, "pe.qkv"),
    ("dve.qkv", 1, "act.qkv"),
    ("pe.ks", 1, "dve.qkv"),
    ("act.ks", 1, "pe.ks"),
    ("dve.ks", 1, "act.ks"),
    ("pe.qs", 1, "dve.qkv"),
    ("act.qs", 1, "pe.qs"),
    ("pe.max", 4, "act.qs", "dve.ks"),
    ("dve.max", 4, "pe.max"),
    ("dve.parts", 1, "dve.max"),
    ("pe.qb", 1, "dve.parts"),
    ("act.qb", 1, "pe.qb"),
    ("pe.exp", 4, "act.qb"),
    ("act.exp", 4, "pe.exp"),
    ("pe.pv", 1, "act.exp"),
    ("act.pv", 1, "pe.pv"),
    ("pe.oT", 1, "act.pv"),
    ("dve.oT", 1, "pe.oT"),
    ("pe.aT", 1, "dve.oT"),
    ("act.aT", 1, "pe.aT"),
    ("pe.wo", 1, "act.aT"),
    ("dve.wo", 1, "pe.wo"),
    ("pool.fnorm", 1, "dve.wo"),
)
STEPS = (
    (("dve.stats", 1), ("pool.norm", 1, "dve.stats")) + ATTENTION + (
        ("dve.qx", 1, "pool.fnorm"),
        ("pe.fxT", 1, "dve.qx"),
        ("act.fxT", 1, "pe.fxT"),
        ("pe.gate", 1, "act.fxT"),
        ("act.gate", 1, "pe.gate"),
        ("dve.z1", 1, "act.gate"),
        ("pe.up", 1, "act.fxT"),
        ("dve.up", 1, "pe.up", "dve.z1"),
        ("dve.qh", 1, "dve.up"),
        ("pe.hT", 1, "dve.qh"),
        ("act.hT", 1, "pe.hT"),
        ("pe.down", 1, "act.hT"),
        ("dve.down", 1, "pe.down"),
    ),
    (("pool.norm", 1),) + ATTENTION + (
        ("pe.mxT", 1, "pool.fnorm"),
        ("act.mxT", 1, "pe.mxT"),
        ("pe.logit", 1, "act.mxT"),
        ("dve.top", 1, "pe.logit"),
        ("act.e", 1, "dve.top"),
        ("dve.comb", 1, "act.e"),
        ("pe.z", 4, "act.mxT"),
        ("act.z", 4, "pe.z"),
        ("pe.y", 2, "act.z"),
        ("dve.y", 2, "pe.y", "dve.comb"),
        ("pool.sum", 1, "dve.y"),
    ),
)
DURATION = (
    {"dve.stats": 0.45, "pool.norm": 4.3, "pe.xT": 0.12, "act.xT": 0.22, "pe.qkv": 0.73, "act.qkv": 0.9,
     "dve.qkv": 1.6, "pe.ks": 0.48, "act.ks": 0.76, "dve.ks": 0.6, "pe.qs": 0.45, "act.qs": 0.9,
     "pe.max": 0.41, "dve.max": 0.6, "dve.parts": 1.08, "pe.qb": 0.48, "act.qb": 0.9, "pe.exp": 0.38,
     "act.exp": 0.48, "pe.pv": 1.21, "act.pv": 0.39, "pe.oT": 0.43, "dve.oT": 0.5, "pe.aT": 0.11,
     "act.aT": 0.12, "pe.wo": 0.22, "dve.wo": 0.81, "pool.fnorm": 4, "dve.qx": 1.5, "pe.fxT": 0.06,
     "act.fxT": 0.19, "pe.gate": 0.22, "act.gate": 1.07, "dve.z1": 0.6, "pe.up": 0.23, "dve.up": 0.42,
     "dve.qh": 1.86, "pe.hT": 0.24, "act.hT": 0.49, "pe.down": 0.23, "dve.down": 1.04},
    {"pool.norm": 4.7, "pe.xT": 0.12, "act.xT": 0.17, "pe.qkv": 0.6, "act.qkv": 0.9, "dve.qkv": 1.6,
     "pe.ks": 0.5, "act.ks": 0.9, "dve.ks": 0.47, "pe.qs": 0.47, "act.qs": 0.9, "pe.max": 0.47,
     "dve.max": 0.53, "dve.parts": 1.02, "pe.qb": 0.55, "act.qb": 0.9, "pe.exp": 0.45, "act.exp": 0.49,
     "pe.pv": 1.15, "act.pv": 0.58, "pe.oT": 0.43, "dve.oT": 0.5, "pe.aT": 0.12, "act.aT": 0.16, "pe.wo": 0.22,
     "dve.wo": 0.8, "pool.fnorm": 4.18, "pe.mxT": 0.15, "act.mxT": 0.22, "pe.logit": 0.08, "dve.top": 1.35,
     "act.e": 0.11, "dve.comb": 1.1, "pe.z": 0.89, "act.z": 1, "pe.y": 2.23, "dve.y": 0.55, "pool.sum": 2.91},
)
FREES = {"max": "dve.max", "gate": "act.gate", "up": "dve.up", "y": "dve.y", "exp": "act.exp", "z": "act.z",
         "xT": "act.xT", "qkv": "dve.qkv", "fxT": "act.fxT", "mxT": "act.mxT", "qb": "act.qb", "ks": "dve.ks",
         "qs": "act.qs", "pv": "act.pv", "oT": "dve.oT", "aT": "act.aT", "wo": "dve.wo", "hT": "act.hT",
         "down": "dve.down", "logit": "dve.top"}
SLOTS = {"act.xT": ((2, "pe.qkv"),), "act.qkv": ((3, "pe.qb"), (2, "pe.ks"), (KSLOTS, "pe.pv")),
         "act.ks": ((KSLOTS, "pe.exp"),), "dve.ks": ((KSLOTS, "pe.exp"),), "act.qs": ((2, "pe.max"),),
         "dve.max": ((2, "dve.parts"),), "act.qb": ((2, "pe.exp"),), "act.exp": ((2, "pe.pv"),),
         "act.pv": ((2, "pe.oT"),), "dve.oT": ((2, "pe.aT"),), "act.aT": ((2, "pe.wo"),)}
LAYER_SLOTS = {"pool.norm": (2, "pe.xT"), "dve.qx": (2, "pe.fxT"),
               "act.fxT": (2, "pe.up"), "act.gate": (1, "dve.up"), "dve.up": (2, "dve.qh"), "act.hT": (2, "pe.down"),
               "act.mxT": (2, "pe.z"), "act.z": (2, "pe.y"), "dve.y": (2, "pool.sum")}
FNORM_SLOT = ((2, "dve.qx"), (2, "pe.mxT"))
FIRST = 3
LATENCY = 0.26
PATIENCE = 0.01
WEIGHT = 5.4
BIAS = (
    {"pool.fnorm": 2, "dve.qh": 11, "act.gate": 39, "pe.qkv": -17, "pe.wo": -2, "dve.oT": -4, "dve.max": 3,
     "act.fxT": -14, "dve.z1": -14, "pe.up": 1, "pe.hT": 1, "act.hT": 2, "pe.down": 2, "dve.down": 1,
     "dve.stats": 18, "act.qb": -19, "dve.parts": -1, "pe.exp": -1, "act.qs": -8, "pe.qs": -31, "act.xT": 22,
     "act.qkv": 44, "pe.oT": 5, "pool.norm": -3, "dve.up": 2, "act.ks": 13, "act.aT": -4, "act.pv": -1,
     "act.exp": 7, "pe.ks": 1},
    {"pe.aT": -5, "act.aT": 1, "pe.mxT": -22, "pe.qs": -1, "act.mxT": -1, "dve.y": -6, "pe.z": 1, "act.e": -31,
     "dve.comb": -1, "act.z": 5, "dve.max": -1, "act.qs": 22, "pe.logit": 2, "pool.norm": -12, "dve.oT": -17,
     "dve.parts": 1, "act.ks": 3, "pool.fnorm": 2, "pe.qkv": -4, "dve.wo": 1, "pe.oT": -7, "pe.pv": -22,
     "pe.exp": 1, "act.qb": 1},
)


def plan():
    number = {unit: n for n, unit in enumerate(UNIT_ORDER)}
    parts = [{s[0]: s[1] for s in steps} for steps in STEPS]
    queues = {}
    for n, (l, b) in enumerate(UNIT_ORDER):
        depth = 0.0
        for name, count, *before in STEPS[l]:
            dur = DURATION[l][name]
            if l == 0 and b < FIRST:
                dur = {"dve.stats": 2.5, "pool.norm": 0.0}.get(name, dur)
            for i in range(count):
                queues.setdefault(name, []).append((n, i, dur, before, n * WEIGHT + depth + BIAS[l].get(name, 0.0)))
            depth += dur * count
    end, free = {}, dict.fromkeys(("pe", "act", "dve", "pool"), 0.0)
    order = {e: [] for e in free}
    fills = {}
    earlier = {}

    def ready(name, n, i, before):
        l, b = UNIT_ORDER[n]
        needs = [(s, n, -(-(i + 1) * parts[l][s] // parts[l][name]) - 1) for s in before]
        for ring, reader in SLOTS.get(name, ()):
            if n >= ring:
                needs.append((reader, n - ring, parts[0][reader] - 1))
        ring, reader = FNORM_SLOT[l] if name == "pool.fnorm" else LAYER_SLOTS.get(name, (NB, None))
        if b >= ring:
            needs.append((reader, number[l, b - ring], parts[l][reader] - 1))
        if name == "pool.norm" and l == 1:
            needs.append(("dve.down", number[0, b], 0))
        if name.startswith("pe."):
            bank = BANK[name[3:]]
            done = fills.setdefault(bank, [])
            ring = 2 if bank in "AB" else 1
            if len(done) >= ring:
                needs.append(done[-ring])
        if (name, n, i) in earlier:
            needs.append(earlier[name, n, i])
        t = 0.0
        for s in needs:
            if s not in end:
                return None
            t = max(t, end[s] + (0.0 if s[0].split(".")[0] == name.split(".")[0] else LATENCY))
        return t

    while any(queues.values()):
        best = None
        for engine in free:
            can = []
            for name, queue in queues.items():
                if queue and name.startswith(engine + "."):
                    n, i, dur, before, rank = queue[0]
                    t = ready(name, n, i, before)
                    if t is not None:
                        can.append((max(t, free[engine]), rank, name, dur))
            if can:
                first = min(can)[0]
                t, rank, name, dur = min((c for c in can if c[0] <= first + PATIENCE), key=lambda c: c[1])
                if best is None or first < best[0]:
                    best = (first, t, name, dur, engine)
        first, t, name, dur, engine = best
        n, i = queues[name].pop(0)[:2]
        free[engine] = end[name, n, i] = t + dur
        order[engine].append((name.split(".")[1], n, i))
        if engine == "pe":
            reader, done = (FREES[name[3:]], n, i), fills[BANK[name[3:]]]
            if done:
                earlier[reader] = done[-1]
            done.append(reader)
    return order


def build(nc, x, ctxT, mask0, mask0T, mask1, mask1T, w0q, w0kv, w0o, w1q, w1kv, w1o, bo,
          wg, wu, wd, m1T, mb1, m2T, mb2, gT, gb, cst, out):
    units, order = UNIT_ORDER, plan()
    number = {unit: n for n, unit in enumerate(units)}
    count, where = {}, {}
    for name, n, i in order["pe"]:
        bank = BANK[name]
        u = units[n][1] if name in PER_BATCH else n
        where[name, u, i] = (bank, count.get(bank, 0))
        count[bank] = count.get(bank, 0) + 1

    with ExitStack() as ctx:
        def sb(name, shape, dt=F32):
            return ctx.enter_context(nc.sbuf_tensor(name, shape, dt))

        def sem(name):
            return ctx.enter_context(nc.semaphore(name))

        banks = {k: [ctx.enter_context(nc.psum_tensor(f"ps_{k}{i}", [P, 512], F32))
                     for i in range(2 if k in "AB" else 1)] for k in "ABPQOX"}
        full = {k: sem(f"full_{k}") for k in banks}
        free = {k: sem(f"free_{k}") for k in banks}

        def psum(name, u, i=0):
            bank, n = where[name, u, i]
            return banks[bank][n % len(banks[bank])]

        def wait_free(eng, name, u, i=0):
            bank, n = where[name, u, i]
            if n + 1 > len(banks[bank]):
                eng.wait_ge(free[bank], n + 1 - len(banks[bank]))

        def wait_full(eng, name, u, i=0):
            bank, n = where[name, u, i]
            eng.wait_ge(full[bank], n + 1)

        def wait_done(eng, name, u, i=0):
            bank, n = where[name, u, i]
            eng.wait_ge(free[bank], n + 1)

        x_sb = sb("x_sb", [P, NB, P])
        xb_sb = sb("xb_sb", [P, NB, P])
        ctx_sb = sb("ctx_sb", [P, NB, P])
        m0_i = sb("m0_i", [P, NB, P], I32)
        m0T_i = sb("m0T_i", [P, NB, P], I32)
        m1_i = sb("m1_i", [P, P], I32)
        m1T_i = sb("m1T_i", [P, P], I32)
        m0_b = sb("m0_b", [P, NB, P], BF16)
        m0T_b = sb("m0T_b", [P, NB, P], BF16)
        m1_b = sb("m1_b", [P, P], BF16)
        m1T_b = sb("m1T_b", [P, P], BF16)
        wq_sb = [sb(f"wq{l}_sb", [P, P]) for l in range(2)]
        wkv_sb = [sb(f"wkv{l}_sb", [P, 2 * P]) for l in range(2)]
        wo_sb = [sb(f"wo{l}_sb", [P, P]) for l in range(2)]
        bo_sb = sb("bo_sb", [P, P])
        wf_sb = sb("wf_sb", [P, 3, INNER])
        wf_q = sb("wf_q", [P, 3, INNER], BF16)
        wf_t = sb("wf_t", [P, INNER])
        wf_sum = sb("wf_sum", [P, 3])
        wf_mean = sb("wf_mean", [P, 3])
        wf_inv = sb("wf_inv", [P, 3])
        wf_gu = sb("wf_gu", [P, 2])
        w1_sb = sb("w1_sb", [P, ZCH, P])
        w2_sb = sb("w2_sb", [P, ZCH, P])
        b1_sb = sb("b1_sb", [P, ZCH])
        b2_sb = sb("b2_sb", [P, E * P])
        b2_f = sb("b2_f", [P, E * P])
        b2_h = sb("b2_h", [P, E * P], BF16)
        b2_p = sb("b2_p", [P, E * P], BF16)
        gT_sb = sb("gT_sb", [P, E])
        gb_sb = sb("gb_sb", [P, E])
        cst_sb = sb("cst_sb", [P, C_N])
        id_b = sb("id_b", [P, P], BF16)
        rows3 = sb("rows3", [P, P], BF16)
        ones = sb("ones", [P, P])
        ident = cst_sb[:, C_ID:C_ID + P]
        iota = cst_sb[:, C_IOTA:C_IOTA + E]

        st6 = sb("st6", [P, 4, NB, 6])
        mv = sb("mv", [P, 4, NB, 2])
        hv = sb("hv", [P, 4, NB, 1])
        ry = sb("ry", [P, 4, NB, 4])
        rt = sb("rt", [P, 4, NB, 3])
        xh = sb("xh", [P, 4, 2, P])

        xT = sb("xT", [P, 2, P])
        qst = sb("qst", [P, 3, GROUPS, MROWS], BF16)
        kst = sb("kst", [P, 2, GROUPS, MROWS], BF16)
        qr = sb("qr", [P, 2, P])
        kr = sb("kr", [P, 2, P])
        v_sb = sb("v_sb", [P, KSLOTS, H, DH + 1])
        qT = sb("qT", [P, 2, GROUPS, P], BF16)
        qmT = sb("qmT", [P, 2, GROUPS, P], BF16)
        kblk = sb("kblk", [P, KSLOTS, GROUPS, 2, P], BF16)
        mx = sb("mx", [P, 2, H])
        nm = sb("nm", [P, 2, H])
        probs = sb("probs", [P, 2, H, P])
        oT_sb = sb("oT_sb", [P, 2, 4 * P])
        rden = sb("rden", [P, 2, H])
        attn = sb("attn", [P, 2, H, DH])
        aT_sb = sb("aT_sb", [P, 2, P])

        fs = sb("fs", [P, NB, 16])
        xr = sb("xr", [P, 2, P])
        xq = sb("xq", [P, 2, P], BF16)
        xqT = sb("xqT", [P, 2, P], BF16)
        th = sb("th", [P, INNER])
        gate_sb = sb("gate_sb", [P, INNER])
        z1 = sb("z1", [P, INNER])
        z2 = sb("z2", [P, 2, INNER])
        hr = sb("hr", [P, INNER])
        hq = sb("hq", [P, 2, INNER], BF16)
        hqT = sb("hqT", [P, 2, 4, P], BF16)

        mxT = sb("mxT", [P, 2, P])
        lg = sb("lg", [P, NB, 4, E])
        top_i = sb("top_i", [P, NB, E], mybir.dt.uint32)
        ls = sb("ls", [P, NB, 12])
        comb = sb("comb", [P, NB, E])
        hid = sb("hid", [P, 2, ZCH, P])
        yc = sb("yc", [P, 2, E, P])
        out_sb = sb("out_sb", [P, 2, P])

        s_cst, s_x, s_ctx, s_w0, s_mask, s_w1, s_wf, s_moe = [
            sem(n) for n in ("cst_in", "x_in", "ctx_in", "w0_in", "mask_in", "w1_in", "wf_in", "moe_in")]
        const_ready = sem("const_ready")
        mask0_ready, mask1_ready = sem("mask0_ready"), sem("mask1_ready")
        s_mask1, s_wo = sem("mask1_in"), sem("wo0_in")
        wsum_ready, wmean_ready, wq_ready = sem("wsum_ready"), sem("wmean_ready"), sem("wq_ready")
        b2_ready = sem("b2_ready")
        stats_ready = [sem(f"stats_ready{k}") for k in range(4)]
        xh_ready = [sem(f"xh_ready{k}") for k in range(4)]
        xh_dve_ready = [sem(f"xh_dve_ready{k}") for k in (0, 3)]
        xb_ready = sem("xb_ready")
        v_ready, qst_ready, kst_ready, kblk_ready, mpart_ready = [
            sem(n) for n in ("v_ready", "qst_ready", "kst_ready", "kblk_ready", "mpart_ready")]
        c_ready, xq_ready, z1_ready, hq_ready = [sem(n) for n in ("c_ready", "xq_ready", "z1_ready", "hq_ready")]
        d_ready, e_ready, out_ready = sem("d_ready"), sem("e_ready"), sem("out_ready")
        last_out_ready = sem("last_out_ready")
        s_out = [sem("out_stored0"), sem("out_stored1")]
        dve_done, pool_done = sem("dve_done"), sem("pool_done")

        def q_parts(n, first, parts):
            return qst[:, n % 3, :, first * PAIR:(first + parts) * PAIR].rearrange("p g (c r) -> p g c r", c=parts)

        def k_parts(n, odd):
            return kst[:, n % 2, :, 0:ROWS].rearrange("p g (c t r) -> p g c t r", c=3, t=2)[:, :, :, odd, :]

        def grp(ap):
            return ap.rearrange("p (g r) -> p g r", g=GROUPS)

        def copies(ap, parts):
            return grp(ap).unsqueeze(2).broadcast_to([P, GROUPS, parts, PAIR])

        def xh_sem(k, b):
            if k == 0:
                return (xh_dve_ready[0], b + 1) if b < FIRST else (xh_ready[0], b + 1 - FIRST)
            return (xh_dve_ready[1], 1) if (k, b) == (3, NB - 1) else (xh_ready[k], b + 1)

        def normalise(eng, chain, k, b):
            h, y, t = hv[:, k, b, 0:1], ry[:, k, b, :], rt[:, k, b, :]
            eng.wait_ge(stats_ready[k], b + 1)
            chain(eng.tensor_scalar(h, mv[:, k, b, 1:2], EPS, 0.5, ALU.add, ALU.mult))
            chain(eng.tensor_scalar(y[:, 0:1].bitcast(I32), h.bitcast(I32), -0.5, MAGIC, ALU.mult, ALU.add))
            for s in range(3):
                chain(eng.tensor_scalar(t[:, s:s + 1], y[:, s:s + 1], y[:, s:s + 1], h, ALU.mult, ALU.mult))
                chain(eng.tensor_scalar(y[:, s + 1:s + 2], t[:, s:s + 1], 1.5, y[:, s:s + 1], ALU.subtract, ALU.mult))
            if b >= 2:
                if k in (0, 2):
                    eng.wait_ge(full["P"], where["xT", number[k // 2, b - 2], 0][1] + 1)
                if k == 3:
                    eng.wait_ge(full["P"], where["mxT", b - 2, 0][1] + 1)
                if k == 1:
                    eng.wait_ge(xq_ready, b - 1)
            eng.tensor_scalar(xh[:, k, b % 2, :], x_sb[:, b, :], mv[:, k, b, 0:1], y[:, 3:4],
                              ALU.subtract, ALU.mult).then_inc(xh_sem(k, b)[0], 1)

        block = ctx.enter_context(nc.Block())

        @block.sync
        def _(sp):
            sp.dma_start(x_sb[:, 0, :], x[0]).then_inc(s_x, 16)
            sp.dma_start(cst_sb[:, :], cst).then_inc(s_cst, 16)
            sp.dma_start(x_sb[:, 1:NB, :], x[1:NB].rearrange("b t d -> t b d")).then_inc(s_x, 16)
            sp.dma_start(m0_i[:, :, :], mask0.rearrange("b q k -> q b k")).then_inc(s_mask, 16)
            sp.dma_start(m0T_i[:, :, :], mask0T).then_inc(s_mask, 16)
            sp.dma_start(m1_i[:, :], mask1).then_inc(s_mask1, 16)
            sp.dma_start(m1T_i[:, :], mask1T).then_inc(s_mask1, 16)
            sp.dma_start(wo_sb[0][:, :], w0o).then_inc(s_wo, 16)
            sp.dma_start(wf_sb[:, 0, :], wg).then_inc(s_wf, 16)
            sp.dma_start(wf_sb[:, 1, :], wu).then_inc(s_wf, 16)
            sp.dma_start(wf_sb[:, 2, :], wd).then_inc(s_wf, 16)
            for dst, src in ((wq_sb[1], w1q), (wkv_sb[1], w1kv), (wo_sb[1], w1o),
                             (bo_sb, bo.partition_broadcast(P))):
                sp.dma_start(dst[:, :], src).then_inc(s_w1, 16)
            sp.dma_start(w1_sb[:, :, :], m1T).then_inc(s_moe, 16)
            sp.dma_start(w2_sb[:, :, :], m2T).then_inc(s_moe, 16)
            sp.dma_start(b1_sb[:, :], mb1).then_inc(s_moe, 16)
            sp.dma_start(b2_sb[0:3, :], mb2.partition_broadcast(3)).then_inc(s_moe, 16)
            sp.dma_start(gT_sb[:, :], gT).then_inc(s_moe, 16)
            sp.dma_start(gb_sb[:, :], gb.partition_broadcast(P)).then_inc(s_moe, 16)
            for b in range(NB):
                sp.wait_ge(*((out_ready, b + 1) if b < NB - 1 else (last_out_ready, 1)))
                sp.dma_start(out[b], out_sb[:, b % 2, :]).then_inc(s_out[b % 2], 16)
            for half in s_out:
                sp.wait_ge(half, 8 * NB)

        @block.gpsimd
        def _(pool):
            done = [0]

            def chain(ins):
                done[0] += 1
                ins.then_inc(pool_done, 1)
                pool.wait_ge(pool_done, done[0])

            pool.memset(ones[:, :], 1.0).then_inc(const_ready, 1)
            pool.memset(kst[:, :, :, ROWS:MROWS], 1.0).then_inc(const_ready, 1)
            pool.memset(v_sb[:, :, :, DH:DH + 1], 1.0).then_inc(const_ready, 1)
            pool.memset(rows3[:, :], 0.0)
            pool.memset(b2_p[:, :], 0.0).then_inc(const_ready, 1)
            pool.wait_ge(const_ready, 4)
            pool.memset(rows3[0:3, :], 1.0).then_inc(const_ready, 1)

            def masks_shared():
                pool.wait_ge(s_mask1, 32)
                for dst, src in ((m1_b, m1_i), (m1T_b, m1T_i)):
                    pool.tensor_scalar(dst[:, :], src[:, :], 0.0, MASKED, ALU.is_equal,
                                       ALU.mult).then_inc(mask1_ready, 1)

            def sum_experts(b):
                y = yc[:, b % 2, :, :]
                wait_done(pool, "y", b, 1)
                for w in (4, 2, 1):
                    chain(pool.tensor_tensor(y[:, 0:w, :], y[:, 0:w, :], y[:, w:2 * w, :], ALU.add))
                if b >= 2:
                    pool.wait_ge(s_out[b % 2], 16 * (b // 2))
                pool.tensor_tensor(out_sb[:, b % 2, :], y[:, 0, :], x_sb[:, b, :], ALU.add).then_inc(out_ready, 1)

            for name, n, _ in order["pool"]:
                l, b = units[n]
                if name == "norm":
                    if l == 1 or b >= FIRST: normalise(pool, chain, 2 * l, b)
                    if (l, b) == (0, 4): masks_shared()
                if name == "fnorm" and (l, b) != (1, NB - 1): normalise(pool, chain, 2 * l + 1, b)
                if name == "sum" and b < NB - 1: sum_experts(b)
                if name == "norm" and l == 1:
                    if b == 0:
                        pool.wait_ge(s_w1, 64)
                    pool.tensor_tensor(xb_sb[:, b, :], x_sb[:, b, :], bo_sb[:, :], ALU.add).then_inc(xb_ready, 1)

        @block.tensor
        def _(pe):
            def filled(mm, name, u, i=0):
                mm.then_inc(full[where[name, u, i][0]], 1)

            def maxima_scores(n, i):
                l, b = units[n]
                o = psum("max", n, i)
                if i == 0:
                    wait_done(pe, "qs", n)
                    wait_done(pe, "ks", n)
                if i == 0 and l == 0:
                    pe.wait_ge(mask0_ready, 2 * (b + 1))
                if i == 0 and (l, b) == (1, 0):
                    pe.wait_ge(mask1_ready, 2)
                wait_free(pe, "max", n, i)
                m = (m0_b[:, b, :] if l == 0 else m1_b[:, :]).unsqueeze(1).broadcast_to([P, 4, P])
                pe.matmul(o[:, :].rearrange("p (h k) -> p h k", h=4), id_b[:, :], m, start=True, stop=False)
                for g in (2 * i, 2 * i + 1):
                    mm = pe.matmul(o[:, 256 * (g % 2):256 * (g % 2) + 256], qT[0:ROWS, n % 2, g, :],
                                   kblk[0:ROWS, n % KSLOTS, g, :, :].rearrange("p a b -> p (a b)"),
                                   start=False, stop=(g % 2 == 1))
                filled(mm, "max", n, i)

            def shifted_scores(n, i):
                l, b = units[n]
                o = psum("exp", n, i)
                if i == 0:
                    wait_done(pe, "qb", n)
                wait_free(pe, "exp", n, i)
                m = (m0T_b[:, b, :] if l == 0 else m1T_b[:, :]).unsqueeze(1).broadcast_to([P, 4, P])
                pe.matmul(o[:, :].rearrange("p (h k) -> p h k", h=4), id_b[:, :], m, start=True, stop=False)
                for h in range(4 * i, 4 * i + 4):
                    mm = pe.matmul(o[:, P * (h % 4):P * (h % 4 + 1)], kblk[0:MROWS, n % KSLOTS, h // 2, h % 2, :],
                                   qmT[0:MROWS, n % 2, h // 2, :], start=False, stop=(h % 4 == 3))
                filled(mm, "exp", n, i)

            def turn(name, u, src, idn, dt=F32):
                wait_free(pe, name, u)
                o = psum(name, u)
                o = o[:, 0:P] if dt == F32 else o[:, 0:P // 2].bitcast(BF16)
                filled(pe.transpose(o, src, idn), name, u)

            def qkv(n):
                l, b = units[n]
                if n == 0:
                    pe.wait_ge(s_w0, 32)
                    pe.wait_ge(s_ctx, 16)
                if (l, b) == (1, 0):
                    pe.wait_ge(s_w1, 64)
                wait_free(pe, "qkv", n)
                o = psum("qkv", n)
                pe.matmul(o[:, P:3 * P], ctx_sb[:, b, :], wkv_sb[l][:, :], start=True, stop=True)
                wait_done(pe, "xT", n)
                filled(pe.matmul(o[:, 0:P], xT[:, n % 2, :], wq_sb[l][:, :], start=True, stop=True), "qkv", n)

            def stack(name, n, src, rows):
                wait_free(pe, name, n)
                o = psum(name, n)[:, :].bitcast(BF16)
                for g in range(GROUPS):
                    mm = pe.transpose(o[0:rows, g * P:(g + 1) * P], src[:, g, 0:rows], id_b[:, :])
                filled(mm, name, n)

            def weighted_values(n):
                wait_free(pe, "pv", n)
                pe.wait_ge(v_ready, n + 1)
                wait_done(pe, "exp", n, 3)
                o = psum("pv", n)
                for h in range(H):
                    j = h % 4
                    mm = pe.matmul(o[32 * j:32 * j + DH + 1, (h // 4) * P:(h // 4 + 1) * P], v_sb[:, n % KSLOTS, h, :],
                                   probs[:, n % 2, h, :], start=True, stop=True)
                filled(mm, "pv", n)

            def turn_outputs(n):
                wait_free(pe, "oT", n)
                wait_done(pe, "pv", n)
                o = psum("oT", n)
                for g in range(4):
                    mm = pe.transpose(o[:, g * P:(g + 1) * P], oT_sb[:, n % 2, g * P:(g + 1) * P], ident)
                filled(mm, "oT", n)

            def project(n):
                wait_free(pe, "wo", n)
                wait_done(pe, "aT", n)
                if n == 0:
                    pe.wait_ge(s_wo, 16)
                filled(pe.matmul(psum("wo", n)[:, 0:P], aT_sb[:, n % 2, :], wo_sb[units[n][0]][:, :],
                                 start=True, stop=True), "wo", n)

            def gate_up(name, b):
                if b == 0:
                    pe.wait_ge(wq_ready, 3)
                wait_done(pe, "fxT", b)
                wait_free(pe, name, b)
                k = ("gate", "up").index(name)
                filled(pe.matmul(psum(name, b)[:, :], xqT[:, b % 2, :], wf_q[:, k, :], start=True, stop=True), name, b)

            def turn_hidden(b):
                wait_free(pe, "hT", b)
                pe.wait_ge(hq_ready, b + 1)
                o = psum("hT", b)[:, 0:256].bitcast(BF16)
                for c in range(4):
                    mm = pe.transpose(o[:, c * P:(c + 1) * P], hq[:, b % 2, c * P:(c + 1) * P], id_b[:, :])
                filled(mm, "hT", b)

            def down(b):
                wait_free(pe, "down", b)
                wait_done(pe, "hT", b)
                for c in range(4):
                    mm = pe.matmul(psum("down", b)[:, 0:P], hqT[:, b % 2, c, :], wf_q[:, 2, c * P:(c + 1) * P],
                                   start=(c == 0), stop=(c == 3))
                filled(mm, "down", b)

            def logits(b):
                if b == 0:
                    pe.wait_ge(s_moe, 96)
                wait_free(pe, "logit", b)
                wait_done(pe, "mxT", b)
                filled(pe.matmul(psum("logit", b)[:, 0:E], mxT[:, b % 2, :], gT_sb[:, :], start=True, stop=True), "logit", b)

            def hidden(b, i):
                if i == 0:
                    wait_done(pe, "mxT", b)
                wait_free(pe, "z", b, i)
                for c in range(4):
                    mm = pe.matmul(psum("z", b, i)[:, c * P:(c + 1) * P], w1_sb[:, 4 * i + c, :], mxT[:, b % 2, :],
                                   start=True, stop=True)
                filled(mm, "z", b, i)

            def experts(b, i):
                if b == 0 and i == 0:
                    pe.wait_ge(b2_ready, 1)
                    pe.wait_ge(const_ready, 5)
                wait_free(pe, "y", b, i)
                o = psum("y", b, i)
                pe.matmul(o[:, :], rows3[:, :], b2_p[:, i * 512:(i + 1) * 512], start=True, stop=False)
                wait_done(pe, "z", b, 2 * i + 1)
                for c in range(8 * i, 8 * i + 8):
                    e = c // 2 - 4 * i
                    mm = pe.matmul(o[:, e * P:(e + 1) * P], hid[:, b % 2, c, :], w2_sb[:, c, :],
                                   start=False, stop=(c == 8 * i + 7))
                filled(mm, "y", b, i)

            pe.wait_ge(s_cst, 16)
            pe.wait_ge(dve_done, 1)
            for name, n, i in order["pe"]:
                l, b = units[n]
                u = b if name in PER_BATCH else n
                if name == "max": maxima_scores(u, i)
                if name == "exp": shifted_scores(u, i)
                if name == "xT":
                    pe.wait_ge(*xh_sem(2 * l, b))
                    turn("xT", u, xh[:, 2 * l, b % 2, :], ident)
                if name == "fxT":
                    pe.wait_ge(xq_ready, u + 1)
                    turn("fxT", u, xq[:, u % 2, :], id_b[:, :], BF16)
                if name == "mxT":
                    pe.wait_ge(*xh_sem(3, u))
                    turn("mxT", u, xh[:, 3, u % 2, :], ident)
                if name == "qkv": qkv(u)
                if name == "ks":
                    pe.wait_ge(kst_ready, u + 1)
                    stack("ks", u, kst[:, u % 2, :, :], MROWS)
                if name == "qs":
                    pe.wait_ge(qst_ready, u + 1)
                    stack("qs", u, qst[:, u % 3, :, :], ROWS)
                if name == "qb":
                    pe.wait_ge(mpart_ready, u + 1)
                    stack("qb", u, qst[:, u % 3, :, :], MROWS)
                if name == "pv": weighted_values(u)
                if name == "oT": turn_outputs(u)
                if name == "aT":
                    wait_done(pe, "oT", u)
                    turn("aT", u, attn[:, u % 2, :, :].rearrange("p h d -> p (h d)"), ident)
                if name == "wo": project(u)
                if name in ("gate", "up"): gate_up(name, u)
                if name == "hT": turn_hidden(u)
                if name == "down": down(u)
                if name == "logit": logits(u)
                if name == "z": hidden(u, i)
                if name == "y": experts(u, i)
                if name == "max" and u == 0 and i == 0:
                    pe.wait_ge(wsum_ready, 3)
                    pe.wait_ge(const_ready, 5)
                    pe.wait_ge(dve_done, 2)
                    pe.matmul(banks["X"][0][:, 0:3], ones[:, :], wf_sum[:, :], start=True, stop=True).then_inc(wmean_ready, 1)

        @block.scalar
        def _(act):
            def freed(ins, name, u, i=0):
                ins.then_inc(free[where[name, u, i][0]], 1)

            def evacuate(dst, name, u, src):
                wait_full(act, name, u)
                ins = act.activation(dst, src, ACT.Copy)
                freed(ins, name, u)

            def high_parts(n):
                wait_full(act, "qkv", n)
                o = psum("qkv", n)
                if n >= 3:
                    act.wait_ge(full["Q"], where["qb", n - 3, 0][1] + 1)
                if n >= 2:
                    act.wait_ge(full["Q"], where["ks", n - 2, 0][1] + 1)
                if n == 0:
                    act.wait_ge(const_ready, 5)
                act.activation(q_parts(n, 0, 3), copies(o[:, 0:P], 3), ACT.Copy)
                act.activation(k_parts(n, 1), copies(o[:, P:2 * P], 3), ACT.Copy)
                if n >= KSLOTS:
                    act.wait_ge(full["O"], where["pv", n - KSLOTS, 0][1] + 1)
                act.activation(v_sb[:, n % KSLOTS, :, 0:DH], o[:, 2 * P:3 * P].rearrange("p (h d) -> p h d", h=H),
                               ACT.Copy).then_inc(v_ready, 1)

            def exps(n, i):
                wait_full(act, "exp", n, i)
                if n >= 2 and i == 0:
                    act.wait_ge(full["O"], where["pv", n - 2, 0][1] + 1)
                ins = act.activation(probs[:, n % 2, 4 * i:4 * i + 4, :],
                                     psum("exp", n, i)[:, :].rearrange("p (h k) -> p h k", h=4),
                                     ACT.Exp, scale=ATTN_SCALE[units[n][0]])
                freed(ins, "exp", n, i)

            def relu(b, i):
                wait_full(act, "z", b, i)
                if b >= 2 and i == 0:
                    act.wait_ge(full["A"], where["y", b - 2, 1][1] + 1)
                for c in range(4):
                    ins = act.activation(hid[:, b % 2, 4 * i + c, :], psum("z", b, i)[:, c * P:(c + 1) * P],
                                         ACT.Relu, bias=b1_sb[:, 4 * i + c:4 * i + c + 1])
                freed(ins, "z", b, i)

            act.dma_start(wq_sb[0][:, :], w0q).then_inc(s_w0, 16)
            act.dma_start(wkv_sb[0][:, :], w0kv).then_inc(s_w0, 16)
            act.dma_start(ctx_sb[:, :, :], ctxT).then_inc(s_ctx, 16)

            for name, n, i in order["act"]:
                u = units[n][1] if name in PER_BATCH or name == "e" else n
                if name == "exp": exps(u, i)
                if name == "xT":
                    if u >= 2:
                        act.wait_ge(full["P"], where["qkv", u - 2, 0][1] + 1)
                    evacuate(xT[:, u % 2, :], "xT", u, psum("xT", u)[:, 0:P])
                if name == "fxT":
                    if u >= 2:
                        act.wait_ge(full["A"], where["up", u - 2, 0][1] + 1)
                    evacuate(xqT[:, u % 2, :], "fxT", u, psum("fxT", u)[:, 0:P // 2].bitcast(BF16))
                if name == "mxT":
                    if u >= 2:
                        act.wait_ge(full["B"], where["z", u - 2, 3][1] + 1)
                    evacuate(mxT[:, u % 2, :], "mxT", u, psum("mxT", u)[:, 0:P])
                if name == "qkv": high_parts(u)
                if name == "qs":
                    if u >= 2:
                        act.wait_ge(full["A"], where["max", u - 2, 3][1] + 1)
                    evacuate(qT[0:ROWS, u % 2, :, :].rearrange("p g k -> p (g k)"), "qs", u,
                             psum("qs", u)[0:ROWS, :].bitcast(BF16))
                if name == "ks":
                    wait_full(act, "ks", u)
                    if u == 0:
                        act.wait_ge(s_cst, 16)
                    if u >= KSLOTS:
                        act.wait_ge(full["B"], where["exp", u - KSLOTS, 3][1] + 1)
                    act.activation(kblk[0:MROWS, u % KSLOTS, :, 0, :],
                                   psum("ks", u)[0:MROWS, :].bitcast(BF16).rearrange("p (g k) -> p g k", g=GROUPS),
                                   ACT.Copy, scale=cst_sb[0:MROWS, C_SEL:C_SEL + 1]).then_inc(kblk_ready, 1)
                if name == "pv":
                    if u >= 2:
                        act.wait_ge(full["O"], where["oT", u - 2, 0][1] + 1)
                    if u == 0:
                        act.wait_ge(const_ready, 5)
                    evacuate(oT_sb[:, u % 2, :], "pv", u, psum("pv", u)[:, :])
                if name == "aT":
                    if u >= 2:
                        act.wait_ge(full["O"], where["wo", u - 2, 0][1] + 1)
                    evacuate(aT_sb[:, u % 2, :], "aT", u, psum("aT", u)[:, 0:P])
                if name == "gate":
                    wait_full(act, "gate", u)
                    act.wait_ge(c_ready, u + 1)
                    if u >= 1:
                        wait_done(act, "up", u - 1)
                    act.activation(th[:, :], psum("gate", u)[:, :], ACT.Tanh, scale=fs[:, u, 4:5])
                    freed(act.activation(gate_sb[:, :], psum("gate", u)[:, :], ACT.Copy), "gate", u)
                if name == "hT":
                    if u >= 2:
                        act.wait_ge(full["X"], where["down", u - 2, 0][1] + 1)
                    evacuate(hqT[:, u % 2, :, :].rearrange("p c t -> p (c t)"), "hT", u,
                             psum("hT", u)[:, 0:256].bitcast(BF16))
                if name == "qb":
                    if u >= 2:
                        act.wait_ge(full["B"], where["exp", u - 2, 3][1] + 1)
                    evacuate(qmT[0:MROWS, u % 2, :, :].rearrange("p g k -> p (g k)"), "qb", u,
                             psum("qb", u)[0:MROWS, :].bitcast(BF16))
                if name == "z": relu(u, i)
                if name == "e":
                    act.wait_ge(d_ready, u + 1)
                    act.activation(ls[:, u, 0:1], ls[:, u, 4:5], ACT.Exp).then_inc(e_ready, 1)

        @block.vector
        def _(dve):
            done = [0]

            def mark(ins):
                done[0] += 1
                ins.then_inc(dve_done, 1)
                return done[0]

            def chain(ins):
                dve.wait_ge(dve_done, mark(ins))

            def freed(ins, name, u, i=0):
                ins.then_inc(free[where[name, u, i][0]], 1)

            def stats(k, b):
                if k == 0 and b < 2:
                    dve.wait_ge(s_x, 16 if b == 0 else 32)
                chain(dve.bn_stats(st6[:, k, b, :], x_sb[:, b, :]))
                dve.bn_aggr(mv[:, k, b, :], st6[:, k, b, :]).then_inc(stats_ready[k], 1)

            def masks(b):
                if b == 0:
                    dve.wait_ge(s_mask, 32)
                for dst, src in ((m0_b, m0_i), (m0T_b, m0T_i)):
                    dve.tensor_scalar(dst[:, b, :], src[:, b, :], 0.0, MASKED, ALU.is_equal,
                                      ALU.mult).then_inc(mask0_ready, 1)

            def low_parts(n):
                o = psum("qkv", n)
                dve.wait_ge(v_ready, n + 1)
                i = n % 2
                q_rest = mark(dve.tensor_tensor(grp(qr[:, i, :]), grp(o[:, 0:P]), q_parts(n, 0, 1)[:, :, 0, :],
                                                ALU.subtract))
                ins = dve.tensor_tensor(grp(kr[:, i, :]), grp(o[:, P:2 * P]), k_parts(n, 1)[:, :, 0, :], ALU.subtract)
                freed(ins, "qkv", n)
                dve.wait_ge(dve_done, q_rest)
                q_mid = mark(dve.tensor_copy(q_parts(n, 3, 2), copies(qr[:, i, :], 2)))
                wait_done(dve, "qkv", n)
                k_mid = mark(dve.tensor_copy(k_parts(n, 0)[:, :, 1:3, :], copies(kr[:, i, :], 2)))
                dve.wait_ge(dve_done, q_mid)
                dve.tensor_tensor(q_parts(n, 5, 1)[:, :, 0, :], grp(qr[:, i, :]), q_parts(n, 3, 1)[:, :, 0, :],
                                  ALU.subtract).then_inc(qst_ready, 1)
                dve.wait_ge(dve_done, k_mid)
                dve.tensor_tensor(k_parts(n, 0)[:, :, 0, :], grp(kr[:, i, :]), k_parts(n, 0)[:, :, 1, :],
                                  ALU.subtract).then_inc(kst_ready, 1)

            def key_blocks(n):
                dve.wait_ge(kblk_ready, n + 1)
                if n >= KSLOTS:
                    dve.wait_ge(full["B"], where["exp", n - KSLOTS, 3][1] + 1)
                freed(dve.tensor_scalar(kblk[0:MROWS, n % KSLOTS, :, 1, :],
                                        psum("ks", n)[0:MROWS, :].bitcast(BF16).rearrange("p (g k) -> p g k", g=GROUPS),
                                        cst_sb[0:MROWS, C_SEL + 1:C_SEL + 2], None, ALU.mult), "ks", n)

            def maxima(n, i):
                wait_full(dve, "max", n, i)
                ins = dve.tensor_reduce(mx[:, n % 2, 4 * i:4 * i + 4],
                                        psum("max", n, i)[:, :].rearrange("p (h k) -> p h k", h=4), AX.X, ALU.max)
                freed(ins, "max", n, i)

            def maxima_parts(n):
                wait_done(dve, "max", n, 3)
                i = n % 2
                st = qst[:, n % 3, :, ROWS:MROWS].rearrange("p g (j c) -> p g j c", j=2)
                hd = lambda ap: ap.rearrange("p (g j) -> p g j", j=2)
                m, rest = hd(mx[:, i, :]), hd(nm[:, i, :])
                chain(dve.tensor_scalar(st[:, :, :, 0], m, -1.0, None, ALU.mult))
                chain(dve.scalar_tensor_tensor(out=rest, in0=m, scalar=-1.0, in1=st[:, :, :, 0],
                                               op0=ALU.mult, op1=ALU.subtract))
                chain(dve.tensor_copy(st[:, :, :, 1], rest))
                dve.tensor_tensor(st[:, :, :, 2], rest, st[:, :, :, 1], ALU.subtract).then_inc(mpart_ready, 1)

            def divide(n):
                wait_full(dve, "oT", n)
                o = psum("oT", n)[:, :].rearrange("p (h r) -> p h r", h=H)
                i = n % 2
                chain(dve.reciprocal(rden[:, i, :].unsqueeze(2), o[:, :, DH:DH + 1]))
                if n >= 2:
                    dve.wait_ge(full["O"], where["aT", n - 2, 0][1] + 1)
                ins = dve.tensor_tensor(attn[:, i, :, :], o[:, :, 0:DH],
                                        rden[:, i, :].unsqueeze(2).broadcast_to([P, H, DH]), ALU.mult)
                freed(ins, "oT", n)

            def add_attention(n):
                l, b = units[n]
                wait_full(dve, "wo", n)
                if l == 1:
                    dve.wait_ge(xb_ready, b + 1)
                res = x_sb[:, b, :] if l == 0 else xb_sb[:, b, :]
                ins = dve.tensor_tensor(x_sb[:, b, :], psum("wo", n)[:, 0:P], res, ALU.add)
                freed(ins, "wo", n)
                wait_done(dve, "wo", n)

            def quantise_x(b):
                i = b % 2
                f = lambda c: fs[:, b, c:c + 1]
                dve.wait_ge(*xh_sem(1, b))
                chain(dve.tensor_reduce(f(0), xh[:, 1, i, :], AX.X, ALU.max, apply_absolute_value=True))
                dve.tensor_scalar(f(2), f(0), EPS, 1.0 / QMAX, ALU.max, ALU.mult)
                chain(dve.tensor_scalar(f(1), f(0), EPS, None, ALU.max))
                if b == 0:
                    dve.wait_ge(wq_ready, 3)
                chain(dve.reciprocal(f(3), f(2)))
                dve.tensor_scalar(f(4), f(1), wf_gu[:, 0:1], None, ALU.mult).then_inc(c_ready, 1)
                dve.tensor_scalar(f(5), f(1), f(1), wf_gu[:, 1:2], ALU.mult, ALU.mult)
                chain(dve.tensor_scalar(xr[:, i, :], xh[:, 1, i, :], f(3), ROUND, ALU.mult, ALU.add))
                if b >= 2:
                    dve.wait_ge(full["P"], where["fxT", b - 2, 0][1] + 1)
                dve.tensor_scalar(xq[:, i, :], xr[:, i, :], ROUND, QMAX, ALU.subtract, ALU.min).then_inc(xq_ready, 1)

            def silu_gate(b):
                wait_done(dve, "gate", b)
                dve.scalar_tensor_tensor(out=z1[:, :], in0=th[:, :], scalar=1.0, in1=gate_sb[:, :],
                                         op0=ALU.add, op1=ALU.mult).then_inc(z1_ready, 1)

            def times_up(b):
                wait_full(dve, "up", b)
                dve.wait_ge(z1_ready, b + 1)
                ins = dve.tensor_tensor(z2[:, b % 2, :], z1[:, :], psum("up", b)[:, :], ALU.mult)
                freed(ins, "up", b)

            def quantise_h(b):
                i = b % 2
                f = lambda c: fs[:, b, c:c + 1]
                wait_done(dve, "up", b)
                chain(dve.tensor_reduce(f(7), z2[:, i, :], AX.X, ALU.max, apply_absolute_value=True))
                chain(dve.tensor_scalar(f(8), f(7), f(5), EPS, ALU.mult, ALU.max))
                dve.tensor_scalar(f(13), f(8), wf_mean[:, 2:3], 1.0 / QMAX, ALU.mult, ALU.mult)
                chain(dve.reciprocal(f(10), f(8)))
                chain(dve.tensor_scalar(f(11), f(10), QMAX, f(5), ALU.mult, ALU.mult))
                chain(dve.tensor_scalar(hr[:, :], z2[:, i, :], f(11), ROUND, ALU.mult, ALU.add))
                if b >= 2:
                    dve.wait_ge(full["X"], where["hT", b - 2, 0][1] + 1)
                dve.tensor_scalar(hq[:, i, :], hr[:, :], ROUND, QMAX, ALU.subtract, ALU.min).then_inc(hq_ready, 1)

            def add_ffn(b):
                wait_full(dve, "down", b)
                ins = dve.scalar_tensor_tensor(out=x_sb[:, b, :], in0=psum("down", b)[:, 0:P], scalar=fs[:, b, 13:14],
                                               in1=x_sb[:, b, :], op0=ALU.mult, op1=ALU.add)
                freed(ins, "down", b)
                wait_done(dve, "down", b)

            def top2(b):
                L = lambda c: lg[:, b, c, :]
                wait_full(dve, "logit", b)
                if b == 0:
                    dve.wait_ge(s_moe, 96)
                ins = dve.tensor_tensor(L(0), psum("logit", b)[:, 0:E], gb_sb[:, :], ALU.add)
                freed(ins, "logit", b)
                wait_done(dve, "logit", b)
                chain(dve.max(L(1), L(0)))
                dve.tensor_tensor(ls[:, b, 4:5], L(1)[:, 1:2], L(1)[:, 0:1], ALU.subtract).then_inc(d_ready, 1)
                chain(dve.max_index(top_i[:, b, :], L(1), L(0)))
                chain(dve.tensor_copy(ls[:, b, 6:8], top_i[:, b, 0:2]))

            def combine(b):
                L = lambda c: lg[:, b, c, :]
                s = lambda c: ls[:, b, c:c + 1]
                dve.wait_ge(e_ready, b + 1)
                chain(dve.tensor_scalar(s(1), s(0), 1.0, None, ALU.add))
                chain(dve.reciprocal(s(2), s(1)))
                second = mark(dve.tensor_scalar(s(3), s(0), s(2), None, ALU.mult))
                dve.tensor_scalar(L(2), iota, s(6), s(2), ALU.is_equal, ALU.mult)
                dve.wait_ge(dve_done, second)
                chain(dve.tensor_scalar(L(3), iota, s(7), s(3), ALU.is_equal, ALU.mult))
                chain(dve.tensor_tensor(comb[:, b, :], L(2), L(3), ALU.add))

            def weigh(b, i):
                wait_full(dve, "y", b, i)
                if b >= 2 and i == 0:
                    dve.wait_ge(out_ready, b - 1)
                freed(dve.tensor_tensor(yc[:, b % 2, 4 * i:4 * i + 4, :],
                                        psum("y", b, i)[:, :].rearrange("p (e o) -> p e o", e=4),
                                        comb[:, b, 4 * i:4 * i + 4].unsqueeze(2).broadcast_to([P, 4, P]),
                                        ALU.mult), "y", b, i)

            def sum_last(i):
                b = NB - 1
                y = yc[:, b % 2, :, :]
                wait_done(dve, "y", b, i)
                e = 4 * i
                chain(dve.tensor_tensor(y[:, e:e + 2, :], y[:, e:e + 2, :], y[:, e + 2:e + 4, :], ALU.add))
                chain(dve.tensor_tensor(y[:, e, :], y[:, e, :], y[:, e + 1, :], ALU.add))
                if i == 0:
                    chain(dve.tensor_tensor(y[:, 0, :], y[:, 0, :], x_sb[:, b, :], ALU.add))
                else:
                    dve.wait_ge(s_out[b % 2], 16 * (b // 2))
                    dve.tensor_tensor(out_sb[:, b % 2, :], y[:, 0, :], y[:, 4, :], ALU.add).then_inc(last_out_ready, 1)

            def sum_weights():
                dve.wait_ge(s_wf, 48)
                for k in range(3):
                    dve.tensor_reduce(wf_sum[:, k:k + 1], wf_sb[:, k, :], AX.X, ALU.add,
                                      apply_absolute_value=True).then_inc(wsum_ready, 1)

            def ternary_weights():
                dve.wait_ge(wmean_ready, 1)
                chain(dve.tensor_scalar(wf_mean[:, :], banks["X"][0][:, 0:3], 1.0 / (P * INNER), EPS, ALU.mult, ALU.max))
                chain(dve.reciprocal(wf_inv[:, :], wf_mean[:, :]))
                dve.tensor_scalar(wf_gu[:, 0:1], wf_mean[:, 0:1], 0.5 / QMAX, None, ALU.mult)
                chain(dve.tensor_scalar(wf_gu[:, 1:2], wf_mean[:, 0:1], wf_mean[:, 1:2], 0.5 / QMAX / QMAX, ALU.mult, ALU.mult))
                for k in range(3):
                    if k:
                        dve.wait_ge(wq_ready, k)
                    chain(dve.tensor_scalar(wf_t[:, :], wf_sb[:, k, :], wf_inv[:, k:k + 1], ROUND, ALU.mult, ALU.add))
                    chain(dve.tensor_scalar(wf_t[:, :], wf_t[:, :], ROUND, 1.0, ALU.subtract, ALU.min))
                    dve.tensor_scalar(wf_q[:, k, :], wf_t[:, :], -1.0, None, ALU.max).then_inc(wq_ready, 1)

            def bias_parts():
                dve.wait_ge(s_moe, 96)
                dve.wait_ge(const_ready, 5)
                r3 = lambda ap: ap[0:3, :]
                for sel, src in ((C_FROM1, b2_sb), (C_FROM2, b2_f)):
                    chain(dve.tensor_copy(r3(b2_h), r3(src)))
                    chain(dve.scalar_tensor_tensor(out=r3(b2_f), in0=r3(b2_h), scalar=r3(cst_sb)[:, sel:sel + 1],
                                                   in1=r3(src), op0=ALU.mult, op1=ALU.add))
                dve.tensor_copy(r3(b2_p), r3(b2_f)).then_inc(b2_ready, 1)

            dve.wait_ge(s_cst, 16)
            mark(dve.tensor_copy(id_b[:, :], ident))
            mark(dve.memset(banks["O"][0][:, :], 0.0))
            stats(0, 0)
            normalise(dve, chain, 0, 0)
            for name, n, i in order["dve"]:
                l, b = units[n]
                if name == "stats" and n:
                    stats(0, b)
                    if b < FIRST: normalise(dve, chain, 0, b)
                if name == "qkv":
                    if (l, b) != (0, 0) and l == 0: masks(b)
                    low_parts(n)
                    if (l, b) == (0, 0): masks(b)
                    if (l, b) == (0, 0): sum_weights()
                    if (l, b) == (0, 1): ternary_weights()
                    if (l, b) == (1, 0): bias_parts()
                if name == "ks": key_blocks(n)
                if name == "max": maxima(n, i)
                if name == "parts": maxima_parts(n)
                if name == "oT": divide(n)
                if name == "wo":
                    add_attention(n)
                    stats(2 * l + 1, b)
                    if (l, b) == (1, NB - 1): normalise(dve, chain, 3, b)
                if name == "qx": quantise_x(b)
                if name == "z1": silu_gate(b)
                if name == "up": times_up(b)
                if name == "qh": quantise_h(b)
                if name == "down":
                    add_ffn(b)
                    stats(2, b)
                if name == "top": top2(b)
                if name == "comb": combine(b)
                if name == "y":
                    weigh(b, i)
                    if b == NB - 1: sum_last(i)


_ORDER = ["x", "ctxT", "mask0", "mask0T", "mask1", "mask1T", "w0q", "w0kv", "w0o", "w1q", "w1kv", "w1o", "bo",
          "wg", "wu", "wd", "m1T", "mb1", "m2T", "mb2", "gT", "gb", "cst"]


def kernel(**inputs):
    import numpy as np
    import concourse.bacc as bacc
    from concourse.bass_utils import run_bass_kernel_spmd

    a = {k: np.asarray(v) for k, v in inputs.items()}

    def per_head(w):
        big = np.zeros((P, P), w.dtype)
        for h in range(H):
            big[h * DH:(h + 1) * DH, h * DH:(h + 1) * DH] = w.T
        return big

    cst = np.zeros((P, C_N), np.float32)
    cst[:, C_ID:C_ID + P] = np.eye(P)
    for r in range(MROWS):
        cst[r, C_SEL + ((r % PAIR) // DH if r < ROWS else (r - ROWS) // 3)] = 1.0
    cst[:, C_IOTA:C_IOTA + E] = np.arange(E)
    cst[1:3, C_FROM1] = -1.0
    cst[2:3, C_FROM2] = -1.0
    data = {
        "x": a["x"],
        "ctxT": a["ctx_1024"].transpose(2, 0, 1),
        "mask0": a["mask_BxSxS2_ik1"],
        "mask0T": a["mask_BxSxS2_ik1"].transpose(2, 0, 1),
        "mask1": a["mask_1x1xSxS2_ik1"][0, 0],
        "mask1T": a["mask_1x1xSxS2_ik1"][0, 0].T,
        "w0q": a["L0_xattn_Wq"].T,
        "w0kv": np.concatenate([a["L0_xattn_Wk"].T, a["L0_xattn_Wv"].T], axis=1),
        "w0o": a["L0_xattn_Wo"].T,
        "w1q": per_head(a["L1_xattn_Wq"]),
        "w1kv": np.concatenate([per_head(a["L1_xattn_Wk"]), per_head(a["L1_xattn_Wv"])], axis=1),
        "w1o": a["L1_xattn_Wo"].T,
        "bo": a["L1_xattn_bo"],
        "wg": a["L0_ffn_w_gate"].T,
        "wu": a["L0_ffn_w_up"].T,
        "wd": a["L0_ffn_w_down"].T.reshape(INNER // P, P, P).transpose(1, 0, 2).reshape(P, INNER),
        "m1T": a["L1_ffn_W1"].reshape(ZCH, P, P).transpose(2, 0, 1),
        "mb1": a["L1_ffn_b1"].reshape(ZCH, P).T,
        "m2T": a["L1_ffn_W2"].transpose(0, 2, 1).reshape(ZCH, P, P).transpose(1, 0, 2),
        "mb2": a["L1_ffn_b2"].reshape(E * P),
        "gT": a["L1_ffn_Wg"].T,
        "gb": a["L1_ffn_bg"],
        "cst": cst,
    }
    nc = bacc.Bacc("TRN2", target_bir_lowering=False, num_devices=1)
    arrays, args = {}, []
    for name in _ORDER:
        v = np.ascontiguousarray(data[name])
        arrays[f"in_{name}"] = v
        args.append(nc.dram_tensor(f"in_{name}", v.shape, mybir.dt.from_np(v.dtype), kind="ExternalInput").ap())
    args.append(nc.dram_tensor("out_y", (NB, P, P), F32, kind="ExternalOutput").ap())
    build(nc, *args)
    r = run_bass_kernel_spmd(nc, [arrays], core_ids=[0])
    return r.results[0]["out_y"]
```
